# Optimizing a Trainium2 kernel written in Bass

```python
import numpy as np
import jax
import jax.numpy as jnp

def _softmax(x, axis=-1):
    return jax.nn.softmax(x, axis=axis)

def _gelu(x):
    return jax.nn.gelu(x, approximate=True)

def _silu(x):
    return jax.nn.silu(x)

def _sigmoid(x):
    return jax.nn.sigmoid(x)

def _layernorm(x, axis=-1, eps=1e-05):
    m = jnp.mean(x, axis=axis, keepdims=True)
    v = jnp.var(x, axis=axis, keepdims=True)
    return (x - m) / jnp.sqrt(v + eps)

def _scatter_add(tgt, idx, src, axis=0):
    return tgt.at[idx].add(src)

def _segment_sum(src, seg, n):
    return jax.ops.segment_sum(src, seg, n)
kernel_name = 'mk_xattn_ffn_d1_seqx_r8_4324cc'

def setup_inputs(seed: int=0):
    np.random.seed(seed)
    _w = jnp.asarray

    def _rec_inputs():
        import jax
        import jax.numpy as jnp
        _rk = jax.random.key(seed)
        x = -0.0002928 + 1 * jax.random.normal(jax.random.fold_in(_rk, 1), (16, 128, 128), jnp.float32)
        _lenS = 128 - jax.random.randint(jax.random.fold_in(_rk, 7), (16,), 0, max(1, 128 // 4) + 1, jnp.int32)
        _lenS2 = 128 - jax.random.randint(jax.random.fold_in(_rk, 8), (16,), 0, max(1, 128 // 4) + 1, jnp.int32)
        _ctx_1024P = jax.random.normal(jax.random.fold_in(_rk, 11), (16, 16, 128), jnp.float32)
        _ctx_1024c = jax.random.dirichlet(jax.random.fold_in(_rk, 511), 0.3 * jnp.ones((16,), jnp.float32), (16, 128))
        _ctx_1024t = jnp.einsum('bsk,bkd->bsd', _ctx_1024c, _ctx_1024P)
        _ctx_1024t = _ctx_1024t * jax.lax.rsqrt(jnp.mean(jnp.square(_ctx_1024t)) + 1e-12) * 0.953939
        ctx_1024 = -1.39393e-06 + 0.999914 * (_ctx_1024t + 0.3 * jax.random.normal(jax.random.fold_in(_rk, 611), (16, 128, 128), jnp.float32))
        return (x, ctx_1024)
    x, ctx_1024 = _rec_inputs()

    def _L0_xattn_setup():
        import jax, jax.numpy as jnp
        import numpy as np
        import math
        H = 16
        D = 128
        DH = D // H
        A = 1000.0

        def _alibi_bias(L, dtype):
            hh = jnp.arange(1, H + 1, dtype=jnp.float32)
            m = jnp.exp(-jnp.power(5000.0, (hh - 1.0) / (H - 1.0) * 0.8))
            seq = jnp.arange(L, dtype=jnp.float32)
            dist = jnp.abs(seq[:, None] - seq[None, :])
            bias = m[:, None, None] * jax.nn.softplus(A + dist)
            return bias.astype(dtype)
        key = jax.random.key(seed)
        ks = jax.random.split(key, 11)
        B, L = (2, 256)
        s = 1.0 / math.sqrt(D)
        inp = {'q': jax.random.normal(ks[0], (B, L, D), jnp.float32), 'k': jax.random.normal(ks[1], (B, L, D), jnp.float32), 'v': jax.random.normal(ks[2], (B, L, D), jnp.float32), 'Wq': jax.random.normal(ks[3], (D, D), jnp.float32) * s, 'bq': jnp.zeros((D,), jnp.float32), 'Wk': jax.random.normal(ks[4], (D, D), jnp.float32) * s, 'bk': jnp.zeros((D,), jnp.float32), 'Wv': jax.random.normal(ks[5], (D, D), jnp.float32) * s, 'bv': jnp.zeros((D,), jnp.float32), 'Wo': jax.random.normal(ks[6], (D, D), jnp.float32) * s, 'bo': jnp.zeros((D,), jnp.float32)}
        return inp
    _L0_xattn_all = _L0_xattn_setup()
    _L0_xattn_in = {k: v for k, v in _L0_xattn_all.items() if k in ('Wq', 'bq', 'Wk', 'bk', 'Wv', 'bv', 'Wo', 'bo')}
    del _L0_xattn_all

    def _L0_ffn_setup():
        import jax, jax.numpy as jnp
        import numpy as np
        B, S, D = (2, 256, 128)
        E, K, F = (16, 2, 64)
        FS = 128
        key = jax.random.key(seed)
        ks = jax.random.split(key, 8)

        def w(k, shape, fan_in):
            return jax.random.normal(k, shape, jnp.float32) / np.sqrt(fan_in).astype(np.float32)
        return {'x': jax.random.normal(ks[0], (B, S, D), jnp.float32), 'Wr': w(ks[1], (D, E), D), 'Wg': w(ks[2], (E, D, F), D), 'Wu': w(ks[3], (E, D, F), D), 'Wd': w(ks[4], (E, F, D), F), 'Sg': w(ks[5], (D, FS), D), 'Su': w(ks[6], (D, FS), D), 'Sd': w(ks[7], (FS, D), FS)}
    _L0_ffn_all = _L0_ffn_setup()
    _L0_ffn_in = {k: v for k, v in _L0_ffn_all.items() if k in ('Wr', 'Wg', 'Wu', 'Wd', 'Sg', 'Su', 'Sd')}
    del _L0_ffn_all
    return {'x': x, 'ctx_1024': ctx_1024, 'L0_xattn_Wq': _L0_xattn_in['Wq'], 'L0_xattn_bq': _L0_xattn_in['bq'], 'L0_xattn_Wk': _L0_xattn_in['Wk'], 'L0_xattn_bk': _L0_xattn_in['bk'], 'L0_xattn_Wv': _L0_xattn_in['Wv'], 'L0_xattn_bv': _L0_xattn_in['bv'], 'L0_xattn_Wo': _L0_xattn_in['Wo'], 'L0_xattn_bo': _L0_xattn_in['bo'], 'L0_ffn_Wr': _L0_ffn_in['Wr'], 'L0_ffn_Wg': _L0_ffn_in['Wg'], 'L0_ffn_Wu': _L0_ffn_in['Wu'], 'L0_ffn_Wd': _L0_ffn_in['Wd'], 'L0_ffn_Sg': _L0_ffn_in['Sg'], 'L0_ffn_Su': _L0_ffn_in['Su'], 'L0_ffn_Sd': _L0_ffn_in['Sd']}

def reference(x, ctx_1024, L0_xattn_Wq, L0_xattn_bq, L0_xattn_Wk, L0_xattn_bk, L0_xattn_Wv, L0_xattn_bv, L0_xattn_Wo, L0_xattn_bo, L0_ffn_Wr, L0_ffn_Wg, L0_ffn_Wu, L0_ffn_Wd, L0_ffn_Sg, L0_ffn_Su, L0_ffn_Sd):
    import jax
    import jax.numpy as jnp

    def _L0_xattn_ref(q, k, v, Wq, bq, Wk, bk, Wv, bv, Wo, bo):
        import jax, jax.numpy as jnp
        import numpy as np
        import math
        H = 16
        D = 128
        DH = D // H
        A = 1000.0

        def _alibi_bias(L, dtype):
            hh = jnp.arange(1, H + 1, dtype=jnp.float32)
            m = jnp.exp(-jnp.power(5000.0, (hh - 1.0) / (H - 1.0) * 0.8))
            seq = jnp.arange(L, dtype=jnp.float32)
            dist = jnp.abs(seq[:, None] - seq[None, :])
            bias = m[:, None, None] * jax.nn.softplus(A + dist)
            return bias.astype(dtype)
        B, L, _ = q.shape

        def proj(x, W, b):
            return (x @ W.T + b).reshape(B, L, H, DH).transpose(0, 2, 1, 3)
        Q = proj(q, Wq, bq)
        K = proj(k, Wk, bk)
        V = proj(v, Wv, bv)
        scores = jnp.einsum('bhid,bhjd->bhij', Q, K) / math.sqrt(DH)
        scores = scores + _alibi_bias(L, scores.dtype)[None]
        attn = jax.nn.softmax(scores, axis=-1)
        x = jnp.einsum('bhij,bhjd->bhid', attn, V)
        x = x.transpose(0, 2, 1, 3).reshape(B, L, D)
        return x @ Wo.T + bo

    def _L0_ffn_ref(x, Wr, Wg, Wu, Wd, Sg, Su, Sd):
        import jax, jax.numpy as jnp
        import numpy as np
        B, S, D = (2, 256, 128)
        E, K, F = (16, 2, 64)
        FS = 128
        b, s, d = x.shape
        T = b * s
        xf = x.reshape(T, d)
        shared = jax.nn.silu(xf @ Sg) * (xf @ Su) @ Sd
        probs = jax.nn.softmax(xf @ Wr, axis=-1)
        topk_p, topk_i = jax.lax.top_k(probs, K)
        n_exp = Wr.shape[1]
        cw = jnp.zeros((T, n_exp), x.dtype).at[jnp.arange(T)[:, None], topk_i].add(topk_p)

        def step(acc, ew):
            wg, wu, wd, c = ew
            y = jax.nn.silu(xf @ wg) * (xf @ wu) @ wd
            return (acc + y * c[:, None], None)
        routed, _ = jax.lax.scan(step, jnp.zeros_like(xf), (Wg, Wu, Wd, cw.T))
        return (routed + shared).reshape(b, s, d)
    x = x + _L0_xattn_ref(_layernorm(x, axis=-1), ctx_1024, ctx_1024, L0_xattn_Wq, L0_xattn_bq, L0_xattn_Wk, L0_xattn_bk, L0_xattn_Wv, L0_xattn_bv, L0_xattn_Wo, L0_xattn_bo)
    x = x + _L0_ffn_ref(_layernorm(x, axis=-1), L0_ffn_Wr, L0_ffn_Wg, L0_ffn_Wu, L0_ffn_Wd, L0_ffn_Sg, L0_ffn_Su, L0_ffn_Sd)
    return x

_drawn_inputs = setup_inputs


def setup_inputs(seed=0):
    import zlib

    import numpy as np

    out = dict(_drawn_inputs(seed))
    spreads = {'L0_xattn_bq': (0.0, 0.1),
     'L0_xattn_bk': (0.0, 0.1),
     'L0_xattn_bv': (0.0, 0.1),
     'L0_xattn_bo': (0.0, 0.1)}
    factors = {}
    for name, (base, spread) in spreads.items():
        noise = np.random.default_rng([zlib.crc32(name.encode()), seed]).standard_normal(out[name].shape)
        drawn = base * np.exp(spread * noise) if base else spread * noise
        out[name] = jnp.asarray(drawn.astype(out[name].dtype))
    for name, factor in factors.items():
        out[name] = (out[name] * factor).astype(out[name].dtype)
    return out
```

```python
from contextlib import ExitStack

import numpy as np
import concourse.bass as bass
from concourse import mybir

F32 = mybir.dt.float32
F32R = mybir.dt.float32r
F16 = mybir.dt.float16
BF16 = mybir.dt.bfloat16
ALU = mybir.AluOpType
ACT = mybir.ActivationFunctionType
AX_X = mybir.AxisListType.X

P = 128
H, DH = 16, 8
HG = 4
NHG = H // HG
NB = 2
T = NB * P
E, FE = 16, 64
NCH = E * FE // P + 1
SHARED = NCH - 1
EPS = 1e-5
BIAS_A = 1000.0
BIAS_SCALE = 16384.0
SPLIT_SLOPES = 7
SMALL_SLOPES = 4
SROWS = 4 * DH
ZROWS = 96
AROWS = ZROWS + 2


def at_start(i):
    return isinstance(i, int) and i == 0


def slopes():
    hh = np.arange(1, H + 1, dtype=np.float32)
    return np.exp(-np.power(np.float32(5000.0), (hh - 1) / (H - 1) * np.float32(0.8))).astype(np.float32)


def constants():
    i = np.arange(P)
    dist = ((BIAS_A + np.abs(i[:, None] - i[None, :])) / BIAS_SCALE).astype(np.float16)
    return {"c_ident": np.eye(P, dtype=np.float32), "c_dist": dist}


def xattn_moe_kernel(nc, x, ctxT, wqkvoT, bqk, bv, bo, wgT, wuT, wd, wr, c_ident, c_dist, out):
    NG = x.shape[1] // NB
    m = slopes().astype(np.float64) * BIAS_SCALE
    m_hi = m.astype(np.float16)
    m_lo = (m - m_hi.astype(np.float64)).astype(np.float16)
    q_scale = float(1.0 / np.sqrt(np.float32(DH)))

    stack = ExitStack()
    with stack:
        def sb(name, shape, dt=F32):
            return stack.enter_context(nc.sbuf_tensor(name, shape, dt))

        def psum(name, shape):
            return stack.enter_context(nc.psum_tensor(name, shape, F32))

        def sem(name):
            return stack.enter_context(nc.semaphore(name))

        x_all = sb("x_all", [P, NG * NB, P])
        x1_all = sb("x1_all", [P, NG * NB, P])
        wT = sb("wT", [P, 4, P])
        bqk_sb = sb("bqk_sb", [P, 2])
        bv_rep, bo_rep = sb("bv_rep", [P, P]), sb("bo_rep", [P, P])
        wg_sb, wu_sb, wd_sb = sb("wg_sb", [P, NCH, P]), sb("wu_sb", [P, NCH, P]), sb("wd_sb", [P, NCH, P])
        wr_sb = sb("wr_sb", [P, E])
        wg_hi, wg_lo = sb("wg_hi", [P, NCH, P], F32R), sb("wg_lo", [P, NCH, P], F32R)
        wu_hi, wu_lo = sb("wu_hi", [P, NCH, P], F32R), sb("wu_lo", [P, NCH, P], F32R)
        wr_hi, wr_lo = sb("wr_hi", [P, E], F32R), sb("wr_lo", [P, E], F32R)
        ident, ident16 = sb("ident", [P, P]), sb("ident16", [P, P], F16)
        dist16 = sb("dist16", [P, P], F16)
        slope_hi = sb("slope_hi", [P, SPLIT_SLOPES, P], F16)
        slope_lo = sb("slope_lo", [P, SPLIT_SLOPES, P], F16)
        slope_small = sb("slope_small", [P, SMALL_SLOPES, P], BF16)
        neg_half, eps_sb = sb("neg_half", [P, NB]), sb("eps_sb", [P, NB])
        ctx_g = sb("ctx_g", [P, T])
        stats1, mv1 = sb("stats1", [P, NB, 6]), sb("mv1", [P, NB, 2])
        ve1, rstd1 = sb("ve1", [P, NB]), sb("rstd1", [P, NB])
        xn, xnT = sb("xn", [P, NB, P]), sb("xnT", [P, T])
        qk_hi, qk_lo = sb("qk_hi", [P, 2, T], F16), sb("qk_lo", [P, 2, T], F16)
        qs, ks = sb("qs", [AROWS, H, T], F16), sb("ks", [AROWS, H, T], F16)
        v_aug = sb("v_aug", [P, NB, 2, 4, 32])
        nmax = sb("nmax", [P, NB, H])
        nsplit = sb("nsplit", [P, NB, 2, H], F16)
        nmT = sb("nmT", [2 * H, NB, P], F16)
        probs = sb("probs", [P, NB, H * P])
        pv_sb = sb("pv_sb", [P, 4 * P])
        rden = sb("rden", [P, 4, 4])
        attn, attnT = sb("attn", [P, P]), sb("attnT", [P, P])
        xb = sb("xb", [P, NB, P])
        stats2, mv2 = sb("stats2", [P, NB, 6]), sb("mv2", [P, NB, 2])
        ve2, rstd2 = sb("ve2", [P, NB]), sb("rstd2", [P, NB])
        x2n = sb("x2n", [P, NB, P])
        x2_hi, x2_lo = sb("x2_hi", [P, T], F32R), sb("x2_lo", [P, T], F32R)
        lmax, lsh, le = sb("lmax", [P, NB]), sb("lsh", [P, NB, E]), sb("le", [P, NB, E])
        lsum, lrec = sb("lsum", [P, NB]), sb("lrec", [P, NB])
        pr = sb("pr", [P, NB, E + 8])
        top8, drop8 = sb("top8", [P, NB, 8]), sb("drop8", [P, NB, 8])
        rest = sb("rest", [P, NB, E + 8])
        cw = sb("cw", [P, NB, E])
        cwT = sb("cwT", [E, T])
        crep = sb("crep", [P, NCH - 1, T])
        th, tg = sb("th", [P, 2, T]), sb("tg", [P, 2, T])
        hid = sb("hid", [P, NCH, T])
        y = sb("y", [P, NB, P])
        carrier = sb("carrier", [P, 1])
        cw_dram = nc.dram_tensor("cw_dram", [NG, E, T], F32, kind="Internal").ap()

        ps_s = [psum("ps_s0", [P, 512]), psum("ps_s1", [P, 512])]
        ps_st = [psum("ps_st0", [P, 512]), psum("ps_st1", [P, 512])]
        ps_pv = psum("ps_pv", [P, 512])
        ps_up = [psum("ps_up0", [P, 2, T]), psum("ps_up1", [P, 2, T])]
        ps_m = psum("ps_m", [P, 512])
        ps_nm = ps_s[0][0:2 * H, 0:P // 2].bitcast(F16)
        ps_qk, ps_v = ps_s[0], ps_s[1][:, 0:T]
        ps_x2T, ps_cwT, ps_dn = ps_m[:, 0:T], ps_m[0:E, 0:T], ps_m[:, 0:T]
        ps_lg, ps_xT = ps_m[:, T:T + NB * E], ps_m[:, T:2 * T]
        ps_aT, ps_o = ps_pv[:, 0:P], ps_pv[:, P:2 * P]

        s_x, s_wqkvo, s_small, s_const, s_wexp = (sem(n) for n in ("s_x", "s_wqkvo", "s_small", "s_const", "s_wexp"))
        s_ctx, s_stack, s_cwd, s_crep, s_out = (sem(n) for n in ("s_ctx", "s_stack", "s_cwd", "s_crep", "s_out"))
        s_nm = [sem("s_nm0"), sem("s_nm1")]
        pool_setup, dve_setup, act_setup = sem("pool_setup"), sem("dve_setup"), sem("act_setup")
        xT_mm, qk_mm, v_mm, s_mm, nm_mm, st_mm, pv_mm, pvT_mm, aT_mm, o_mm, x2T_mm, lg_mm, cwT_mm, up_mm, dn_mm = (
            sem(n) for n in ("xT_mm", "qk_mm", "v_mm", "s_mm", "nm_mm", "st_mm", "pv_mm", "pvT_mm", "aT_mm", "o_mm",
                             "x2T_mm", "lg_mm", "cwT_mm", "up_mm", "dn_mm"))
        xT_sb, qkhi_sb, nm_sb, exp_sb, pvev_sb, aT_sb, x2hi_sb, lexp_sb, cwT_sb, tanh_sb = (
            sem(n) for n in ("xT_sb", "qkhi_sb", "nm_sb", "exp_sb", "pvev_sb", "aT_sb", "x2hi_sb", "lexp_sb", "cwT_sb",
                             "tanh_sb"))
        st1_sb, mv1_sb, xn_sb, qklo_sb, v_sb, max_sb, nh_sb, ns_sb, rden_sb, attn_sb, x1_sb, st2_sb, mv2_sb, x2n_sb = (
            sem(n) for n in ("st1_sb", "mv1_sb", "xn_sb", "qklo_sb", "v_sb", "max_sb", "nh_sb", "ns_sb", "rden_sb",
                             "attn_sb", "x1_sb", "st2_sb", "mv2_sb", "x2n_sb"))
        x2lo_sb, lmax_sb, lsh_sb, route_sb, cw_sb, tg_sb, hid_sb, y_sb = (
            sem(n) for n in ("x2lo_sb", "lmax_sb", "lsh_sb", "route_sb", "cw_sb", "tg_sb", "hid_sb", "y_sb"))
        ve1_sb, rstd1_sb, xb_sb, ve2_sb, rstd2_sb, hc_sb = (
            sem(n) for n in ("ve1_sb", "rstd1_sb", "xb_sb", "ve2_sb", "rstd2_sb", "hc_sb"))
        own = sem("pool_own")
        stack_pads = sem("stack_pads")
        ROUTE = 6

        def run_steps(eng, step):
            step(None, None, 0)
            step(None, 0, 1)
            step(0, 1, 2)
            with eng.Fori(1, NG - 2) as k:
                step(k, k + 1, k + 2)
            step(NG - 2, NG - 1, None)
            step(NG - 1, None, None)

        block = stack.enter_context(nc.Block())

        @block.sync
        def _(sp):
            def load_ctx(p):
                if not at_start(p):
                    sp.wait_ge(v_mm, p)
                sp.dma_start(ctx_g[:], ctxT[:, bass.ds(p * T, T)]).then_inc(s_ctx, 16)

            def stacks(p):
                if not at_start(p):
                    sp.wait_ge(st_mm, 2 * NHG * p)
                sp.wait_ge(qkhi_sb, 2 * p + 2)
                sp.wait_ge(qklo_sb, 2 * p + 2)
                if at_start(p):
                    sp.wait_ge(stack_pads, 3)
                for t, (a, b) in enumerate(((qk_hi, qk_hi), (qk_hi, qk_lo), (qk_lo, qk_hi), (qk_lo, qk_lo))):
                    sp.dma_start(qs[DH * t:DH * (t + 1), :, :], a[:, 0, :]).then_inc(s_stack, 16)
                    sp.dma_start(ks[DH * t:DH * (t + 1), :, :], b[:, 1, :]).then_inc(s_stack, 16)

            def shift_rows(a, b):
                sp.wait_ge(nm_sb, 2 * a + b + 1)
                sp.dma_start(qs[ZROWS:AROWS, :, b * P:(b + 1) * P], nmT[:, b, :]).then_inc(s_nm[b], 16)

            def spread_weights(f):
                sp.wait_ge(cwT_sb, f + 1)
                if not at_start(f):
                    sp.wait_ge(dn_mm, f)
                sp.dma_start(cw_dram[f], cwT[:]).then_inc(s_cwd, 16)
                sp.wait_ge(s_cwd, 16 * f + 16)
                for odd in range(2):
                    src = bass.AP(cw_dram.tensor, f * (E * T) + odd * T, [[0, FE], [2 * T, E // 2], [1, T]])
                    sp.dma_start(crep[FE * odd:FE * (odd + 1), :, :], src).then_inc(s_crep, 16)

            def store(f):
                sp.wait_ge(y_sb, f + 1)
                sp.dma_start(out[:, bass.ds(f * NB, NB), :], y[:]).then_inc(s_out, 16)

            def step(f, a, p):
                if p is not None:
                    load_ctx(p)
                if a is not None:
                    shift_rows(a, 0)
                if f is not None:
                    spread_weights(f)
                if a is not None:
                    shift_rows(a, 1)
                if p is not None:
                    stacks(p)
                if f is not None:
                    store(f)

            sp.dma_start(x_all[:, 0:NB, :], x[:, 0:NB, :]).then_inc(s_x, 16)
            sp.dma_start(ident[:], c_ident).then_inc(s_const, 16)
            sp.dma_start(wT[:], wqkvoT).then_inc(s_wqkvo, 16)
            sp.dma_start(bqk_sb[:], bqk).then_inc(s_wqkvo, 16)
            sp.dma_start(dist16[:], c_dist).then_inc(s_const, 16)
            sp.dma_start(bv_rep[:], bass.AP(bv.tensor, 0, [[0, P], [1, P]])).then_inc(s_small, 16)
            sp.dma_start(bo_rep[:], bass.AP(bo.tensor, 0, [[0, P], [1, P]])).then_inc(s_small, 16)
            step(None, None, 0)
            sp.wait_ge(s_x, 16)
            sp.dma_start(x_all[:, NB:, :], x[:, NB:, :]).then_inc(s_x, 16)
            sp.dma_start(wg_sb[:], wgT).then_inc(s_wexp, 16)
            sp.dma_start(wu_sb[:], wuT).then_inc(s_wexp, 16)
            sp.dma_start(wr_sb[:], wr).then_inc(s_wexp, 16)
            sp.dma_start(wd_sb[:], wd).then_inc(s_wexp, 16)
            step(None, 0, 1)
            step(0, 1, 2)
            with sp.Fori(1, NG - 2) as k:
                step(k, k + 1, k + 2)
            step(NG - 2, NG - 1, None)
            step(NG - 1, None, None)
            sp.wait_ge(s_out, 16 * NG)

        @block.tensor
        def _(pe):
            mm = nc.tensor.matmul

            def project_x(p):
                pe.wait_ge(xn_sb, p + 1)
                if at_start(p):
                    pe.wait_ge(s_const, 32)
                for b in range(NB):
                    last = nc.tensor.transpose(ps_xT[:, b * P:(b + 1) * P], xn[:, b, :], ident[:])
                last.then_inc(xT_mm, 1)

            def project_qk(p):
                pe.wait_ge(xT_sb, p + 1)
                pe.wait_ge(s_ctx, 16 * p + 16)
                if at_start(p):
                    pe.wait_ge(dve_setup, 2)
                    pe.wait_ge(s_wqkvo, 32)
                else:
                    pe.wait_ge(max_sb, 2 * NHG * p - 1)
                    pe.wait_ge(nm_sb, 2 * p)
                mm(ps_qk[:, 0:T], wT[:, 0, :], xnT[:], start=True, stop=True)
                mm(ps_qk[:, T:2 * T], wT[:, 1, :], ctx_g[:], start=True, stop=True).then_inc(qk_mm, 1)

            def project_v(p):
                if not at_start(p):
                    pe.wait_ge(max_sb, 2 * NHG * p)
                for b in range(NB):
                    last = mm(ps_v[:, b * P:(b + 1) * P], ctx_g[:, b * P:(b + 1) * P], wT[:, 2, :], start=True, stop=True)
                last.then_inc(v_mm, 1)

            def scores(a, b, g):
                bank, n = ps_s[g % 2], 2 * NHG * a + NHG * b + g
                if b == 0 and g == 0:
                    pe.wait_ge(s_stack, 128 * a + 128)
                    if at_start(a):
                        pe.wait_ge(own, 8)
                        pe.wait_ge(stack_pads, 3)
                elif b == 0 and g == 1:
                    pe.wait_ge(v_sb, a + 1)
                else:
                    pe.wait_ge(max_sb, n - 1)
                    if b == 1 and g == 0:
                        pe.wait_ge(nm_sb, 2 * a + 1)
                if g == 0:
                    mm(bank[:], dist16[:], slope_hi[:, 0:HG, :], start=True, stop=False, skip_group_check=True)
                for h in range(HG * g, HG * g + HG):
                    o = (h - HG * g) * P
                    last = mm(bank[:, o:o + P], qs[0:ZROWS, h, b * P:(b + 1) * P], ks[0:ZROWS, h, b * P:(b + 1) * P],
                              start=(g > 0), stop=True, skip_group_check=True)
                last.then_inc(s_mm, 1)

            def shift_T(a, b):
                pe.wait_ge(ns_sb, 2 * a + b + 1)
                nc.tensor.transpose(ps_nm, nsplit[:, b, :, :].rearrange("p s h -> p (s h)"), ident16[:]).then_inc(nm_mm, 1)

            def scores_T(a, b, g):
                bank = ps_st[g % 2]
                if at_start(a) and b == 0:
                    if g >= 2:
                        pe.wait_ge(exp_sb, g - 1)
                else:
                    pe.wait_ge(exp_sb, 2 * NHG * a + NHG * b + g - 1)
                if g == 0:
                    pe.wait_ge(s_nm[b], 16 * a + 16)
                h0, first = HG * g, True
                n_split = min(max(SPLIT_SLOPES - h0, 0), HG)
                n_small = min(max(SPLIT_SLOPES + SMALL_SLOPES - h0, 0), HG) - n_split
                if n_split:
                    for part in (slope_hi, slope_lo):
                        mm(bank[:, 0:n_split * P], dist16[:], part[:, h0:h0 + n_split, :], start=first, stop=False,
                           skip_group_check=True)
                        first = False
                if n_small:
                    j = h0 + n_split - SPLIT_SLOPES
                    mm(bank[:, n_split * P:(n_split + n_small) * P], dist16[:], slope_small[:, j:j + n_small, :],
                       start=first, stop=False, skip_group_check=True)
                    first = False
                for h in range(h0, h0 + HG):
                    o = (h - h0) * P
                    last = mm(bank[:, o:o + P], ks[:, h, b * P:(b + 1) * P], qs[:, h, b * P:(b + 1) * P],
                              start=first, stop=True, skip_group_check=True)
                    first = False
                last.then_inc(st_mm, 1)

            def weigh_values(a, b):
                pe.wait_ge(exp_sb, 2 * NHG * a + NHG * (b + 1))
                if b == 0:
                    pe.wait_ge(v_sb, a + 1)
                if not (at_start(a) and b == 0):
                    pe.wait_ge(x1_sb, 2 * a + b)
                for r in range(2):
                    n = (3, 1)[r]
                    for c in range(4):
                        h = 3 * c if r == 0 else 12 + c
                        last = mm(ps_pv[32 * c:32 * c + 32, r * 3 * P:(r * 3 + n) * P], v_aug[:, b, r, c, :],
                                  probs[:, b, h * P:(h + n) * P], start=True, stop=True, skip_group_check=True)
                last.then_inc(pv_mm, 1)

            def values_T(a, b):
                pe.wait_ge(pvev_sb, 2 * a + b + 1)
                for l in range(4):
                    last = nc.tensor.transpose(ps_pv[:, l * P:(l + 1) * P], pv_sb[:, l * P:(l + 1) * P], ident[:])
                last.then_inc(pvT_mm, 1)

            def attention_T(a, b):
                pe.wait_ge(attn_sb, 2 * a + b + 1)
                nc.tensor.transpose(ps_aT, attn[:], ident[:]).then_inc(aT_mm, 1)

            def project_out(a, b):
                pe.wait_ge(aT_sb, 2 * a + b + 1)
                mm(ps_o, attnT[:], wT[:, 3, :], start=True, stop=True).then_inc(o_mm, 1)

            def expert_in_T(f):
                pe.wait_ge(x2n_sb, f + 1)
                if not at_start(f):
                    pe.wait_ge(y_sb, f)
                for b in range(NB):
                    last = nc.tensor.transpose(ps_x2T[:, b * P:(b + 1) * P], x2n[:, b, :], ident[:])
                last.then_inc(x2T_mm, 1)

            def router(f):
                pe.wait_ge(x2hi_sb, f + 1)
                pe.wait_ge(x2lo_sb, f + 1)
                if at_start(f):
                    pe.wait_ge(act_setup, 3)
                    pe.wait_ge(dve_setup, 5)
                for b in range(NB):
                    for n, (u, w) in enumerate(((x2_lo, wr_hi), (x2_hi, wr_lo), (x2_hi, wr_hi))):
                        last = mm(ps_lg[:, b * E:(b + 1) * E], u[:, b * P:(b + 1) * P], w[:], start=(n == 0), stop=(n == 2))
                last.then_inc(lg_mm, 1)

            def weights_T(f):
                pe.wait_ge(cw_sb, f + 1)
                for b in range(NB):
                    last = nc.tensor.transpose(ps_cwT[:, b * P:(b + 1) * P], cw[:, b, :], ident[:])
                last.then_inc(cwT_mm, 1)

            def up(f, c):
                if not (at_start(f) and c < 2):
                    pe.wait_ge(hid_sb, NCH * f + max(c - 1, 0))
                for k, (hi, lo) in enumerate(((wg_hi, wg_lo), (wu_hi, wu_lo))):
                    for n, (w, u) in enumerate(((lo, x2_hi), (hi, x2_lo), (hi, x2_hi))):
                        last = mm(ps_up[c % 2][:, k, :], w[:, c, :], u[:], start=(n == 0), stop=(n == 2))
                last.then_inc(up_mm, 1)

            def down(f, chunks):
                if chunks[0] == 0 and at_start(f):
                    pe.wait_ge(pool_setup, 1)
                for c in chunks:
                    if c == SHARED:
                        pe.wait_ge(hid_sb, NCH * f + NCH)
                    elif c % 2 == 0:
                        pe.wait_ge(hc_sb, (NCH - 1) // 2 * f + c // 2 + 1)
                    for b in range(NB):
                        last = mm(ps_dn[:, b * P:(b + 1) * P], hid[:, c, b * P:(b + 1) * P], wd_sb[:, c, :],
                                  start=(c == 0 and b == 0), stop=(c == SHARED), skip_group_check=True)
                if chunks[-1] == SHARED:
                    last.then_inc(dn_mm, 1)

            def step(f, a, p):
                fs, as_, ps = f is not None, a is not None, p is not None
                if as_:
                    scores(a, 0, 0)
                    scores(a, 0, 1)
                if fs: expert_in_T(f)
                if as_: scores(a, 0, 2)
                if fs: router(f)
                if as_: scores(a, 0, 3)
                if fs: up(f, 0)
                if as_: shift_T(a, 0)
                if fs:
                    up(f, 1)
                    up(f, 2)
                for g in range(NHG):
                    if as_:
                        scores_T(a, 0, g)
                        scores(a, 1, g)
                    if fs:
                        if g == 1: weights_T(f)
                        up(f, 3 + g)
                if as_: shift_T(a, 1)
                if ps: project_x(p)
                if as_: weigh_values(a, 0)
                if fs: up(f, 7)
                if ps:
                    project_qk(p)
                    project_v(p)
                if as_: values_T(a, 0)
                if fs: up(f, 8)
                if as_:
                    scores_T(a, 1, 0)
                    attention_T(a, 0)
                    scores_T(a, 1, 1)
                    project_out(a, 0)
                    scores_T(a, 1, 2)
                if fs: down(f, range(0, 2))
                if as_: scores_T(a, 1, 3)
                if fs: down(f, range(2, 6))
                if as_: weigh_values(a, 1)
                if fs: down(f, range(6, NCH))
                if as_:
                    values_T(a, 1)
                    attention_T(a, 1)
                    project_out(a, 1)

            run_steps(pe, step)

        @block.scalar
        def _(act):
            fn = nc.scalar.activation

            def x_T(p):
                act.wait_ge(xT_mm, p + 1)
                fn(xnT[:], ps_xT, ACT.Copy).then_inc(xT_sb, 1)

            def qk_high(p):
                act.wait_ge(qk_mm, p + 1)
                if at_start(p):
                    act.wait_ge(dve_setup, 2)
                else:
                    act.wait_ge(s_stack, 128 * p)
                for k in range(2):
                    fn(qk_hi[:, k, :], ps_qk[:, k * T:(k + 1) * T], ACT.Identity, bias=bqk_sb[:, k:k + 1]).then_inc(qkhi_sb, 1)

            def shift_copy(a, b):
                act.wait_ge(nm_mm, 2 * a + b + 1)
                if not at_start(a):
                    act.wait_ge(s_nm[b], 16 * a)
                fn(nmT[:, b, :], ps_nm, ACT.Copy).then_inc(nm_sb, 1)

            def exponential(a, b, g):
                act.wait_ge(st_mm, 2 * NHG * a + NHG * b + g + 1)
                if g == 0 and not at_start(a):
                    act.wait_ge(pv_mm, 2 * a + b - 1)
                fn(probs[:, b, g * HG * P:(g + 1) * HG * P], ps_st[g % 2][:], ACT.Exp).then_inc(exp_sb, 1)

            def values_copy(a, b):
                act.wait_ge(pv_mm, 2 * a + b + 1)
                if not (at_start(a) and b == 0):
                    act.wait_ge(pvT_mm, 2 * a + b)
                fn(pv_sb[:], ps_pv[:], ACT.Copy).then_inc(pvev_sb, 1)

            def attention_copy(a, b):
                act.wait_ge(aT_mm, 2 * a + b + 1)
                if not (at_start(a) and b == 0):
                    act.wait_ge(o_mm, 2 * a + b)
                fn(attnT[:], ps_aT, ACT.Copy).then_inc(aT_sb, 1)

            def x2_high(f):
                act.wait_ge(x2T_mm, f + 1)
                if not at_start(f):
                    act.wait_ge(up_mm, NCH * f)
                fn(x2_hi[:], ps_x2T, ACT.Copy).then_inc(x2hi_sb, 1)

            def router_exp(f):
                act.wait_ge(lsh_sb, f + 1)
                if not at_start(f):
                    act.wait_ge(route_sb, ROUTE * f)
                fn(le[:], lsh[:], ACT.Exp).then_inc(lexp_sb, 1)

            def weights_copy(f):
                act.wait_ge(cwT_mm, f + 1)
                if not at_start(f):
                    act.wait_ge(s_cwd, 16 * f)
                fn(cwT[:], ps_cwT, ACT.Copy).then_inc(cwT_sb, 1)

            def tanh(f, c):
                act.wait_ge(up_mm, NCH * f + c + 1)
                if not (at_start(f) and c < 2):
                    act.wait_ge(tg_sb, NCH * f + max(c - 1, 0))
                fn(th[:, c % 2, :], ps_up[c % 2][:, 0, :], ACT.Tanh, scale=0.5).then_inc(tanh_sb, 1)

            def step(f, a, p):
                fs, as_, ps = f is not None, a is not None, p is not None
                if fs:
                    x2_high(f)
                    router_exp(f)
                    tanh(f, 0)
                if as_: shift_copy(a, 0)
                if fs:
                    tanh(f, 1)
                    tanh(f, 2)
                for g in range(NHG):
                    if as_: exponential(a, 0, g)
                    if fs:
                        if g == 1: weights_copy(f)
                        tanh(f, 3 + g)
                if as_: shift_copy(a, 1)
                if ps: x_T(p)
                if as_: values_copy(a, 0)
                if fs: tanh(f, 7)
                if ps: qk_high(p)
                if fs: tanh(f, 8)
                if as_:
                    exponential(a, 1, 0)
                    attention_copy(a, 0)
                    for g in range(1, NHG):
                        exponential(a, 1, g)
                    values_copy(a, 1)
                    attention_copy(a, 1)

            nc.scalar.preload_act_table(ACT.Exp)
            step(None, None, 0)
            act.wait_ge(s_wexp, 64)
            fn(wg_hi[:], wg_sb[:], ACT.Copy).then_inc(act_setup, 1)
            fn(wu_hi[:], wu_sb[:], ACT.Copy).then_inc(act_setup, 1)
            fn(wr_hi[:], wr_sb[:], ACT.Copy).then_inc(act_setup, 1)
            step(None, 0, 1)
            step(0, 1, 2)
            with act.Fori(1, NG - 2) as k:
                step(k, k + 1, k + 2)
            step(NG - 2, NG - 1, None)
            step(NG - 1, None, None)

        @block.vector
        def _(dve):
            v = nc.vector

            def carry_wait():
                v.memset(carrier[:], 0.0)

            def norm1_stats(p):
                if at_start(p):
                    dve.wait_ge(s_x, 16)
                elif isinstance(p, int) and p == 1:
                    dve.wait_ge(s_x, 32)
                for b in range(NB):
                    v.bn_stats(stats1[:, b, :], x_all[:, p * NB + b, :]).then_inc(st1_sb, 1)
                dve.wait_ge(st1_sb, NB * p + NB)
                if not at_start(p):
                    dve.wait_ge(ve1_sb, p)
                carry_wait()
                for b in range(NB):
                    v.bn_aggr(mv1[:, b, :], stats1[:, b, :]).then_inc(mv1_sb, 1)

            def norm1(p):
                dve.wait_ge(rstd1_sb, p + 1)
                dve.wait_ge(mv1_sb, NB * p + NB)
                if not at_start(p):
                    dve.wait_ge(xT_mm, p)
                for b in range(NB):
                    last = v.tensor_scalar(xn[:, b, :], x_all[:, p * NB + b, :], mv1[:, b, 0:1], rstd1[:, b:b + 1],
                                           ALU.subtract, ALU.mult)
                last.then_inc(xn_sb, 1)

            def qk_low(p):
                dve.wait_ge(qkhi_sb, 2 * p + 2)
                if not at_start(p):
                    dve.wait_ge(s_stack, 128 * p)
                for k in range(2):
                    v.scalar_tensor_tensor(out=qk_lo[:, k, :], in0=ps_qk[:, k * T:(k + 1) * T], scalar=bqk_sb[:, k:k + 1],
                                           in1=qk_hi[:, k, :], op0=ALU.add, op1=ALU.subtract).then_inc(qklo_sb, 1)

            def values(p):
                dve.wait_ge(v_mm, p + 1)
                if not at_start(p):
                    dve.wait_ge(pv_mm, 2 * p)
                for b in range(NB):
                    for r, (h0, n) in enumerate(((0, 3), (12, 1))):
                        w = n * DH
                        src = ps_v[:, b * P + h0 * DH:b * P + h0 * DH + 4 * w].rearrange("p (c w) -> p c w", c=4)
                        bias = bv_rep[:, h0 * DH:h0 * DH + 4 * w].rearrange("p (c w) -> p c w", c=4)
                        last = v.tensor_tensor(v_aug[:, b, r, :, 0:w], src, bias, ALU.add)
                last.then_inc(v_sb, 1)

            def row_max(a, b, g):
                dve.wait_ge(s_mm, 2 * NHG * a + NHG * b + g + 1)
                v.tensor_reduce(nmax[:, b, HG * g:HG * g + HG], ps_s[g % 2][:].rearrange("p (h j) -> p h j", h=HG), AX_X, ALU.max,
                                negate=True).then_inc(max_sb, 1)

            def split_max(a, b):
                dve.wait_ge(max_sb, 2 * NHG * a + NHG * (b + 1))
                if not at_start(a):
                    dve.wait_ge(nm_mm, 2 * a + b - 1)
                v.tensor_copy(nsplit[:, b, 0, :], nmax[:, b, :]).then_inc(nh_sb, 1)
                dve.wait_ge(nh_sb, 2 * a + b + 1)
                v.tensor_tensor(nsplit[:, b, 1, :], nmax[:, b, :], nsplit[:, b, 0, :], ALU.subtract).then_inc(ns_sb, 1)

            def normalise(a, b):
                dve.wait_ge(pvT_mm, 2 * a + b + 1)
                row = ps_pv[:].ap[0]
                v.reciprocal(rden[:], bass.AP(ps_pv, 24, [list(row), [P, 4], [32, 4]])).then_inc(rden_sb, 1)
                dve.wait_ge(rden_sb, 2 * a + b + 1)
                if not (at_start(a) and b == 0):
                    dve.wait_ge(aT_mm, 2 * a + b)
                v.tensor_tensor(attn[:, 0:96].rearrange("p (c l d) -> p l c d", c=4, l=3),
                                bass.AP(ps_pv, 0, [list(row), [P + DH, 3], [32, 4], [1, DH]]),
                                rden[:, 0:3, :].unsqueeze(3).to_broadcast([P, 3, 4, DH]), ALU.mult)
                v.tensor_tensor(attn[:, 96:128].rearrange("p (c d) -> p c d", c=4),
                                bass.AP(ps_pv, 3 * P, [list(row), [32, 4], [1, DH]]),
                                rden[:, 3, :].unsqueeze(2).to_broadcast([P, 4, DH]), ALU.mult).then_inc(attn_sb, 1)

            def residual1(a, b):
                dve.wait_ge(o_mm, 2 * a + b + 1)
                dve.wait_ge(xb_sb, a + 1)
                v.tensor_tensor(x1_all[:, a * NB + b, :], ps_o, xb[:, b, :], ALU.add).then_inc(x1_sb, 1)

            def norm2_stats(a):
                dve.wait_ge(x1_sb, 2 * a + 2)
                carry_wait()
                for b in range(NB):
                    v.bn_stats(stats2[:, b, :], x1_all[:, a * NB + b, :]).then_inc(st2_sb, 1)
                dve.wait_ge(st2_sb, NB * a + NB)
                if not at_start(a):
                    dve.wait_ge(ve2_sb, a)
                carry_wait()
                for b in range(NB):
                    v.bn_aggr(mv2[:, b, :], stats2[:, b, :]).then_inc(mv2_sb, 1)

            def norm2(a):
                dve.wait_ge(rstd2_sb, a + 1)
                dve.wait_ge(mv2_sb, NB * a + NB)
                if not at_start(a):
                    dve.wait_ge(x2T_mm, a)
                for b in range(NB):
                    last = v.tensor_scalar(x2n[:, b, :], x1_all[:, a * NB + b, :], mv2[:, b, 0:1], rstd2[:, b:b + 1],
                                           ALU.subtract, ALU.mult)
                last.then_inc(x2n_sb, 1)

            def x2_low(f):
                dve.wait_ge(x2hi_sb, f + 1)
                if not at_start(f):
                    dve.wait_ge(up_mm, NCH * f)
                v.tensor_tensor(x2_lo[:], ps_x2T, x2_hi[:].bitcast(F32), ALU.subtract).then_inc(x2lo_sb, 1)

            def router_shift(f):
                dve.wait_ge(lg_mm, f + 1)
                lg = ps_lg.rearrange("p (b e) -> p b e", b=NB)
                if not at_start(f):
                    dve.wait_ge(lexp_sb, f)
                v.tensor_reduce(lmax[:], lg, AX_X, ALU.max).then_inc(lmax_sb, 1)
                dve.wait_ge(lmax_sb, f + 1)
                v.tensor_tensor(lsh[:], lg, lmax[:].unsqueeze(2).to_broadcast([P, NB, E]), ALU.subtract).then_inc(lsh_sb, 1)

            def route(f):
                n = [0]

                def link(ins):
                    n[0] += 1
                    ins.then_inc(route_sb, 1)
                    dve.wait_ge(route_sb, ROUTE * f + n[0])

                dve.wait_ge(lexp_sb, f + 1)
                link(v.tensor_reduce(lsum[:], le[:], AX_X, ALU.add))
                link(v.reciprocal(lrec[:], lsum[:]))
                link(v.tensor_tensor(pr[:, :, 0:E], le[:], lrec[:].unsqueeze(2).to_broadcast([P, NB, E]), ALU.mult))
                carry_wait()
                for b in range(NB):
                    last = v.max(top8[:, b, :], pr[:, b, 0:E])
                link(last)
                link(v.tensor_copy(drop8[:, :, 0:2], top8[:, :, 0:2]))
                carry_wait()
                for b in range(NB):
                    last = v.match_replace(rest[:, b, :], drop8[:, b, :], pr[:, b, :], 0.0)
                link(last)
                if not at_start(f):
                    dve.wait_ge(cwT_mm, f)
                v.tensor_tensor(cw[:], pr[:, :, 0:E], rest[:, :, 0:E], ALU.subtract).then_inc(cw_sb, 1)

            def gate(f, c):
                dve.wait_ge(tanh_sb, NCH * f + c + 1)
                v.scalar_tensor_tensor(out=tg[:, c % 2, :], in0=th[:, c % 2, :], scalar=1.0, in1=ps_up[c % 2][:, 0, :],
                                       op0=ALU.add, op1=ALU.mult).then_inc(tg_sb, 1)
                dve.wait_ge(tg_sb, NCH * f + c + 1)
                if c == 0 and not at_start(f):
                    dve.wait_ge(dn_mm, f)
                v.tensor_tensor(hid[:, c, :], tg[:, c % 2, :], ps_up[c % 2][:, 1, :], ALU.mult).then_inc(hid_sb, 1)

            def residual2(f):
                dve.wait_ge(dn_mm, f + 1)
                if not at_start(f):
                    dve.wait_ge(s_out, 16 * f)
                v.tensor_tensor(y[:], ps_dn.rearrange("p (b d) -> p b d", b=NB), x1_all[:, bass.ds(f * NB, NB), :],
                                ALU.add).then_inc(y_sb, 1)

            def step(f, a, p):
                fs, as_, ps = f is not None, a is not None, p is not None
                if as_:
                    row_max(a, 0, 0)
                    row_max(a, 0, 1)
                if fs: x2_low(f)
                if as_: row_max(a, 0, 2)
                if fs: router_shift(f)
                if as_:
                    row_max(a, 0, 3)
                    split_max(a, 0)
                if fs:
                    gate(f, 0)
                    route(f)
                if ps: norm1_stats(p)
                if fs:
                    gate(f, 1)
                    gate(f, 2)
                for g in range(NHG):
                    if as_: row_max(a, 1, g)
                    if ps and g == 1: norm1(p)
                    if as_ and g == NHG - 1: split_max(a, 1)
                    if fs: gate(f, 3 + g)
                if fs: gate(f, 7)
                if as_: normalise(a, 0)
                if ps: qk_low(p)
                if fs: gate(f, 8)
                if as_:
                    residual1(a, 0)
                if ps: values(p)
                if as_:
                    normalise(a, 1)
                    residual1(a, 1)
                    norm2_stats(a)
                if fs: residual2(f)
                if as_: norm2(a)

            v.memset(qs[0:ZROWS, :, :].bitcast(F32), 0.0).then_inc(stack_pads, 1)
            v.memset(ks[0:ZROWS, :, :].bitcast(F32), 0.0).then_inc(stack_pads, 1)
            v.memset(ks[ZROWS:AROWS, :, :], 1.0).then_inc(stack_pads, 1)
            dve.wait_ge(s_wqkvo, 32)
            v.tensor_scalar(wT[:, 0, :], wT[:, 0, :], q_scale, None, ALU.mult).then_inc(dve_setup, 1)
            v.tensor_scalar(bqk_sb[:, 0:1], bqk_sb[:, 0:1], q_scale, None, ALU.mult).then_inc(dve_setup, 1)
            step(None, None, 0)
            dve.wait_ge(act_setup, 3)
            v.tensor_tensor(wg_lo[:], wg_sb[:], wg_hi[:].bitcast(F32), ALU.subtract).then_inc(dve_setup, 1)
            v.tensor_tensor(wu_lo[:], wu_sb[:], wu_hi[:].bitcast(F32), ALU.subtract).then_inc(dve_setup, 1)
            v.tensor_tensor(wr_lo[:], wr_sb[:], wr_hi[:].bitcast(F32), ALU.subtract).then_inc(dve_setup, 1)
            step(None, 0, 1)
            step(0, 1, 2)
            with dve.Fori(1, NG - 2) as k:
                step(k, k + 1, k + 2)
            step(NG - 2, NG - 1, None)
            step(NG - 1, None, None)

        @block.gpsimd
        def _(pool):
            g = nc.gpsimd

            def inverse_deviation(i, mv, mv_sb, ve, ve_sb, rstd, rstd_sb, used):
                pool.wait_ge(mv_sb, NB * i + NB)
                g.tensor_tensor(ve[:], mv[:, :, 1], eps_sb[:], ALU.add).then_inc(ve_sb, 1)
                pool.wait_ge(ve_sb, i + 1)
                if not at_start(i):
                    pool.wait_ge(used, i)
                g.tensor_tensor(rstd[:], ve[:], neg_half[:], ALU.pow).then_inc(rstd_sb, 1)

            def add_bo(a):
                if at_start(a):
                    pool.wait_ge(s_small, 32)
                    pool.wait_ge(s_x, 32)
                else:
                    pool.wait_ge(x1_sb, 2 * a)
                for b in range(NB):
                    last = g.tensor_tensor(xb[:, b, :], x_all[:, a * NB + b, :], bo_rep[:], ALU.add)
                last.then_inc(xb_sb, 1)

            def weigh_experts(f, pair):
                if pair == 0:
                    pool.wait_ge(s_crep, 32 * f + 32)
                pool.wait_ge(hid_sb, NCH * f + 2 * pair + 2)
                h2, c2 = hid[:, 2 * pair:2 * pair + 2, :], crep[:, 2 * pair:2 * pair + 2, :]
                g.tensor_tensor(h2, h2, c2, ALU.mult).then_inc(hc_sb, 1)

            def step(f, a, p):
                if p is not None:
                    inverse_deviation(p, mv1, mv1_sb, ve1, ve1_sb, rstd1, rstd1_sb, xn_sb)
                if a is not None:
                    add_bo(a)
                if f is not None:
                    for pair in range((NCH - 1) // 2):
                        weigh_experts(f, pair)
                if a is not None:
                    inverse_deviation(a, mv2, mv2_sb, ve2, ve2_sb, rstd2, rstd2_sb, x2n_sb)

            g.memset(neg_half[:], -0.5).then_inc(own, 1)
            g.memset(eps_sb[:], EPS).then_inc(own, 1)
            g.memset(v_aug[:], 1.0).then_inc(own, 1)
            g.memset(pr[:, :, E:], -1.0).then_inc(own, 1)
            g.memset(drop8[:], -1.0).then_inc(own, 1)
            pool.wait_ge(own, 5)
            g.memset(v_aug[:, :, 1, :, DH:3 * DH], 0.0).then_inc(own, 1)
            pool.wait_ge(s_const, 32)
            g.tensor_copy(ident16[:], ident[:]).then_inc(own, 1)
            pool.wait_ge(own, 7)
            step(None, None, 0)
            for h in range(SPLIT_SLOPES):
                g.tensor_scalar(slope_hi[:, h, :], ident[:], float(m_hi[h]), None, ALU.mult)
            for h in range(SPLIT_SLOPES):
                g.tensor_scalar(slope_lo[:, h, :], ident[:], float(m_lo[h]), None, ALU.mult)
            for j in range(SMALL_SLOPES):
                last = g.tensor_scalar(slope_small[:, j, :], ident[:], float(m[SPLIT_SLOPES + j]), None, ALU.mult)
            last.then_inc(own, 1)
            pool.wait_ge(s_wexp, 64)
            g.tensor_scalar(wd_sb[:], wd_sb[:], 0.5, None, ALU.mult).then_inc(pool_setup, 1)
            step(None, 0, 1)
            step(0, 1, 2)
            with pool.Fori(1, NG - 2) as k:
                step(k, k + 1, k + 2)
            step(NG - 2, NG - 1, None)
            step(NG - 1, None, None)


def kernel(x, ctx_1024, L0_xattn_Wq, L0_xattn_bq, L0_xattn_Wk, L0_xattn_bk, L0_xattn_Wv, L0_xattn_bv, L0_xattn_Wo,
           L0_xattn_bo, L0_ffn_Wr, L0_ffn_Wg, L0_ffn_Wu, L0_ffn_Wd, L0_ffn_Sg, L0_ffn_Su, L0_ffn_Sd):
    import numpy as np
    import concourse.bacc as bacc
    from concourse.bass_utils import run_bass_kernel_spmd

    def rows(a):
        return np.ascontiguousarray(a)

    def by_dim(w):
        return np.asarray(w).reshape(H, DH, -1).transpose(2, 1, 0).reshape(P, P)

    x, ctx = np.asarray(x), np.asarray(ctx_1024)
    B = x.shape[0]
    arrays = {
        "x": rows(x.transpose(1, 0, 2)),
        "ctxT": rows(ctx.transpose(2, 0, 1).reshape(P, B * P)),
        "wqkvoT": rows(np.stack([by_dim(L0_xattn_Wq), by_dim(L0_xattn_Wk), np.asarray(L0_xattn_Wv).T,
                                 np.asarray(L0_xattn_Wo).T], axis=1)),
        "bqk": rows(np.stack([np.asarray(b).reshape(H, DH).T.reshape(P) for b in (L0_xattn_bq, L0_xattn_bk)], axis=1)),
        "bv": rows(L0_xattn_bv), "bo": rows(L0_xattn_bo),
        "wgT": rows(np.concatenate([np.asarray(L0_ffn_Wg).transpose(1, 0, 2).reshape(P, E * FE), np.asarray(L0_ffn_Sg)],
                                   axis=1).reshape(P, NCH, P)),
        "wuT": rows(np.concatenate([np.asarray(L0_ffn_Wu).transpose(1, 0, 2).reshape(P, E * FE), np.asarray(L0_ffn_Su)],
                                   axis=1).reshape(P, NCH, P)),
        "wd": rows(np.concatenate([np.asarray(L0_ffn_Wd).reshape(E * FE, P), np.asarray(L0_ffn_Sd)],
                                  axis=0).reshape(NCH, P, P).transpose(1, 0, 2)),
        "wr": rows(L0_ffn_Wr),
        **constants(),
    }
    nc = bacc.Bacc("TRN2", target_bir_lowering=False, num_devices=1)
    aps = {n: nc.dram_tensor(f"in_{n}", a.shape, mybir.dt.from_np(a.dtype), kind="ExternalInput").ap()
           for n, a in arrays.items()}
    out = nc.dram_tensor("out_y", (P, B, P), F32, kind="ExternalOutput").ap()
    xattn_moe_kernel(nc, out=out, **aps)
    r = run_bass_kernel_spmd(nc, [{f"in_{n}": a for n, a in arrays.items()}], core_ids=[0])
    return r.results[0]["out_y"].transpose(1, 0, 2)
```

```python
from contextlib import ExitStack

import numpy as np
import concourse.bass as bass
from concourse import mybir

F32 = mybir.dt.float32
F32R = mybir.dt.float32r
F16 = mybir.dt.float16
BF16 = mybir.dt.bfloat16
ALU = mybir.AluOpType
ACT = mybir.ActivationFunctionType
AX_X = mybir.AxisListType.X

P = 128
H, DH = 16, 8
HG = 4
NHG = H // HG
NB = 2
T = NB * P
E, FE = 16, 64
NCH = E * FE // P + 1
SHARED = NCH - 1
PAIRS = SHARED // 2
EPS = 1e-5
BIAS_A = 1000.0
BIAS_SCALE = 16384.0
SPLIT_SLOPES = 7
SMALL_SLOPES = 4
SROWS = 4 * DH
ZROWS = 96
AROWS = ZROWS + 2


def at_start(i):
    return isinstance(i, int) and i == 0


def slopes():
    hh = np.arange(1, H + 1, dtype=np.float32)
    return np.exp(-np.power(np.float32(5000.0), (hh - 1) / (H - 1) * np.float32(0.8))).astype(np.float32)


def constants():
    i = np.arange(P)
    dist = ((BIAS_A + np.abs(i[:, None] - i[None, :])) / BIAS_SCALE).astype(np.float16)
    return {"c_ident": np.eye(P, dtype=np.float32), "c_dist": dist}


def xattn_moe_kernel(nc, x, ctxT, wqkvoT, bqk, bv, bo, wgT, wuT, wd, wr, c_ident, c_dist, out):
    NG = x.shape[1] // NB
    m = slopes().astype(np.float64) * BIAS_SCALE
    m_hi = m.astype(np.float16)
    m_lo = (m - m_hi.astype(np.float64)).astype(np.float16)
    two_ones = float(np.array([1, 1], np.float16).view(np.float32)[0])
    q_scale = float(1.0 / np.sqrt(np.float32(DH)))

    stack = ExitStack()
    with stack:
        def sb(name, shape, dt=F32):
            return stack.enter_context(nc.sbuf_tensor(name, shape, dt))

        def psum(name, shape):
            return stack.enter_context(nc.psum_tensor(name, shape, F32))

        def sem(name):
            return stack.enter_context(nc.semaphore(name))

        x_all = sb("x_all", [P, NG * NB, P])
        x1_all = sb("x1_all", [P, NG * NB, P])
        wT = sb("wT", [P, 4, P])
        bqk_sb = sb("bqk_sb", [P, 2])
        bv_rep, bo_rep = sb("bv_rep", [P, P]), sb("bo_rep", [P, P])
        wg_sb, wu_sb, wd_sb = sb("wg_sb", [P, NCH, P]), sb("wu_sb", [P, NCH, P]), sb("wd_sb", [P, NCH, P])
        wr_sb = sb("wr_sb", [P, E])
        wg_hi, wg_lo = sb("wg_hi", [P, NCH, P], F32R), sb("wg_lo", [P, NCH, P], F32R)
        wu_hi, wu_lo = sb("wu_hi", [P, NCH, P], F32R), sb("wu_lo", [P, NCH, P], F32R)
        wr_hi, wr_lo = sb("wr_hi", [P, E], F32R), sb("wr_lo", [P, E], F32R)
        ident, ident16 = sb("ident", [P, P]), sb("ident16", [P, P], F16)
        dist16 = sb("dist16", [P, P], F16)
        slope_hi = sb("slope_hi", [P, SPLIT_SLOPES, P], F16)
        slope_lo = sb("slope_lo", [P, SPLIT_SLOPES, P], F16)
        slope_small = sb("slope_small", [P, SMALL_SLOPES, P], BF16)
        neg_half, eps_sb = sb("neg_half", [P, NB]), sb("eps_sb", [P, NB])
        ctx_all = sb("ctx_all", [P, NG * T])
        ctx_g = sb("ctx_g", [P, T])
        stats1, mv1 = sb("stats1", [P, NB, 6]), sb("mv1", [P, NB, 2])
        ve1, rstd1 = sb("ve1", [P, NB]), sb("rstd1", [P, NB])
        xn, xnT = sb("xn", [P, NB, P]), sb("xnT", [P, T])
        qk_parts = sb("qk_parts", [P, 4, 2, T], F16)
        stacks_sb = sb("stacks_sb", [AROWS, H, 2, T], F16)
        qs, ks = stacks_sb[:, :, 0], stacks_sb[:, :, 1]
        v_aug = sb("v_aug", [P, NB, 2, 4, 32])
        nmax = sb("nmax", [P, NB, H])
        nsplit = sb("nsplit", [P, NB, 2, H], F16)
        nmT = sb("nmT", [2 * H, NB, P], F16)
        probs = sb("probs", [P, NB, H * P])
        pv_sb = sb("pv_sb", [P, 4 * P])
        rden = sb("rden", [P, 4, 4])
        attn, attnT = sb("attn", [P, P]), sb("attnT", [P, P])
        xb = sb("xb", [P, NB, P])
        stats2, mv2 = sb("stats2", [P, NB, 6]), sb("mv2", [P, NB, 2])
        ve2, rstd2 = sb("ve2", [P, NB]), sb("rstd2", [P, NB])
        x2n = sb("x2n", [P, NB, P])
        x2_hi, x2_lo = sb("x2_hi", [P, T], F32R), sb("x2_lo", [P, T], F32R)
        lmax, lsh, le = sb("lmax", [P, NB]), sb("lsh", [P, NB, E]), sb("le", [P, NB, E])
        lsum, lrec = sb("lsum", [P, NB]), sb("lrec", [P, NB])
        pr = sb("pr", [P, NB, E + 8])
        top8, drop8 = sb("top8", [P, NB, 8]), sb("drop8", [P, NB, 8])
        rest = sb("rest", [P, NB, E + 8])
        cw = sb("cw", [P, NB, E])
        cwT = sb("cwT", [E, T])
        crep = sb("crep", [P, NCH - 1, T])
        th, tg = sb("th", [P, 2, T]), sb("tg", [P, 2, T])
        hid = sb("hid", [P, NCH, T])
        carrier, pool_carrier = sb("carrier", [P, 1]), sb("pool_carrier", [P, 2])
        cw_dram = nc.dram_tensor("cw_dram", [NG, E, T], F32, kind="Internal").ap()

        ps_s = [psum("ps_s0", [P, 512]), psum("ps_s1", [P, 512])]
        ps_st = [psum("ps_st0", [P, 512]), psum("ps_st1", [P, 512])]
        ps_pv = psum("ps_pv", [P, 512])
        ps_up = [psum("ps_up0", [P, 2, T]), psum("ps_up1", [P, 2, T])]
        ps_m = psum("ps_m", [P, 512])
        ps_nm = ps_pv[0:2 * H, T:T + P // 2].bitcast(F16)
        ps_qk, ps_v = ps_st[1], ps_s[1][:, 0:T]
        ps_x2T, ps_lg, ps_cwT = ps_st[0][:, 0:T], ps_st[0][:, T:T + NB * E], ps_pv[0:E, 0:T]
        ps_xT = ps_s[0][:, T:2 * T]
        ps_dn, ps_aT, ps_o = ps_m[:, 0:T], ps_m[:, T:T + P], ps_m[:, T + P:2 * T]

        s_x, s_wqkvo, s_small, s_const, s_wexp = (sem(n) for n in ("s_x", "s_wqkvo", "s_small", "s_const", "s_wexp"))
        s_ctx, s_stack, s_cwd, s_crep, s_out = (sem(n) for n in ("s_ctx", "s_stack", "s_cwd", "s_crep", "s_out"))
        s_nm = [sem("s_nm0"), sem("s_nm1")]
        pool_setup, dve_setup, act_setup = sem("pool_setup"), sem("dve_setup"), sem("act_setup")
        xT_mm, qk_mm, v_mm, s_mm, nm_mm, st_mm, pv_mm, pvT_mm, aT_mm, o_mm, x2T_mm, lg_mm, cwT_mm, up_mm, dn_mm = (
            sem(n) for n in ("xT_mm", "qk_mm", "v_mm", "s_mm", "nm_mm", "st_mm", "pv_mm", "pvT_mm", "aT_mm", "o_mm",
                             "x2T_mm", "lg_mm", "cwT_mm", "up_mm", "dn_mm"))
        xT_sb, qkhi_sb, nm_sb, exp_sb, pvev_sb, aT_sb, x2hi_sb, lexp_sb, cwT_sb, tanh_sb = (
            sem(n) for n in ("xT_sb", "qkhi_sb", "nm_sb", "exp_sb", "pvev_sb", "aT_sb", "x2hi_sb", "lexp_sb", "cwT_sb",
                             "tanh_sb"))
        st1_sb, mv1_sb, xn_sb, qklo_sb, v_sb, max_sb, nh_sb, ns_sb, rden_sb, attn_sb, x1_sb, st2_sb, mv2_sb, x2n_sb = (
            sem(n) for n in ("st1_sb", "mv1_sb", "xn_sb", "qklo_sb", "v_sb", "max_sb", "nh_sb", "ns_sb", "rden_sb",
                             "attn_sb", "x1_sb", "st2_sb", "mv2_sb", "x2n_sb"))
        x2lo_sb, lmax_sb, lsh_sb, route_sb, cw_sb, tg_sb, hid_sb, y_sb = (
            sem(n) for n in ("x2lo_sb", "lmax_sb", "lsh_sb", "route_sb", "cw_sb", "tg_sb", "hid_sb", "y_sb"))
        ve1_sb, rstd1_sb, xb_sb, ve2_sb, rstd2_sb, hc_sb, pairs_sb, ctx_sb = (
            sem(n) for n in ("ve1_sb", "rstd1_sb", "xb_sb", "ve2_sb", "rstd2_sb", "hc_sb", "pairs_sb", "ctx_sb"))
        own = sem("pool_own")
        first_pairs = sem("first_pairs")
        stack_pads = sem("stack_pads")
        ROUTE = 6

        def run_steps(eng, step):
            step(0, 1, 2, 3)
            with eng.Fori(0, (NG - 4) // 2) as turn:
                for k in range(1, 3):
                    step(*(turn * 2 + (k + i) for i in range(4)))
            step(NG - 3, NG - 2, NG - 1, None)
            step(NG - 2, NG - 1, None, None)

        block = stack.enter_context(nc.Block())

        @block.sync
        def _(sp):
            def stacks(p):
                if at_start(p):
                    sp.wait_ge(first_pairs, 3)
                else:
                    sp.wait_ge(st_mm, 2 * NHG * p)
                for t in range(4):
                    sp.dma_start(stacks_sb[DH * t:DH * (t + 1)].rearrange("d h k t -> d h (k t)"),
                                 qk_parts[:, t].rearrange("p k t -> p (k t)")).then_inc(s_stack, 16)

            def shift_rows(a, b):
                sp.wait_ge(nm_sb, 2 * a + b + 1)
                sp.dma_start(qs[ZROWS:AROWS, :, b * P:(b + 1) * P], nmT[:, b, :]).then_inc(s_nm[b], 16)

            def spread_weights(f):
                if not at_start(f):
                    sp.wait_ge(hc_sb, PAIRS * f)
                sp.wait_ge(cwT_sb, f + 1)
                sp.dma_start(cw_dram[f], cwT[:]).then_inc(s_cwd, 16)
                sp.wait_ge(s_cwd, 16 * f + 16)
                for odd in range(2):
                    src = bass.AP(cw_dram.tensor, f * (E * T) + odd * T, [[0, FE], [2 * T, E // 2], [1, T]])
                    sp.dma_start(crep[FE * odd:FE * (odd + 1), :, :], src).then_inc(s_crep, 16)

            def store(f):
                sp.wait_ge(y_sb, f + 1)
                sp.dma_start(out[:, bass.ds(f * NB, NB), :], x1_all[:, bass.ds(f * NB, NB), :]).then_inc(s_out, 16)

            def step(f, a, p, q):
                if a is not None:
                    shift_rows(a, 0)
                    shift_rows(a, 1)
                if f is not None:
                    spread_weights(f)
                if f is not None and not at_start(f):
                    store(f - 1)
                if p is not None:
                    stacks(p)

            sp.dma_start(x_all[:, 0:2 * NB, :], x[:, 0:2 * NB, :]).then_inc(s_x, 16)
            sp.dma_start(ident[:], c_ident).then_inc(s_const, 16)
            sp.dma_start(wT[:], wqkvoT).then_inc(s_wqkvo, 16)
            sp.dma_start(bqk_sb[:], bqk).then_inc(s_wqkvo, 16)
            sp.dma_start(ctx_all[:, 0:2 * T], ctxT[:, 0:2 * T]).then_inc(s_ctx, 16)
            sp.dma_start(dist16[:], c_dist).then_inc(s_const, 16)
            sp.dma_start(bv_rep[:], bass.AP(bv.tensor, 0, [[0, P], [1, P]])).then_inc(s_small, 16)
            sp.dma_start(bo_rep[:], bass.AP(bo.tensor, 0, [[0, P], [1, P]])).then_inc(s_small, 16)
            step(None, None, None, 0)
            step(None, None, 0, 1)
            step(None, 0, 1, 2)
            run_steps(sp, step)
            spread_weights(NG - 1)
            store(NG - 2)
            store(NG - 1)
            sp.wait_ge(s_out, 16 * NG)

        @block.tensor
        def _(pe):
            mm = nc.tensor.matmul

            def project_x(p):
                pe.wait_ge(xn_sb, p + 1)
                if at_start(p):
                    pe.wait_ge(s_const, 32)
                for b in range(NB):
                    last = nc.tensor.transpose(ps_xT[:, b * P:(b + 1) * P], xn[:, b, :], ident[:])
                last.then_inc(xT_mm, 1)

            def project_q(p):
                pe.wait_ge(xT_sb, p + 1)
                if at_start(p):
                    pe.wait_ge(dve_setup, 2)
                    pe.wait_ge(s_wqkvo, 32)
                mm(ps_qk[:, 0:T], wT[:, 0, :], xnT[:], start=True, stop=True)

            def project_k(p):
                if at_start(p):
                    pe.wait_ge(s_ctx, 16)
                elif isinstance(p, int) and p == 2:
                    pe.wait_ge(s_ctx, 32)
                mm(ps_qk[:, T:2 * T], wT[:, 1, :], ctx_all[:, bass.ds(p * T, T)], start=True, stop=True).then_inc(qk_mm, 1)

            def project_v(p):
                pe.wait_ge(ctx_sb, p + 1)
                if not at_start(p):
                    pe.wait_ge(max_sb, 2 * NHG * p)
                for b in range(NB):
                    last = mm(ps_v[:, b * P:(b + 1) * P], ctx_g[:, b * P:(b + 1) * P], wT[:, 2, :], start=True, stop=True)
                last.then_inc(v_mm, 1)

            def scores(a, b, g, p=None):
                bank, n = ps_s[g % 2], 2 * NHG * a + NHG * b + g
                if b == 0 and g == 0:
                    pe.wait_ge(s_stack, 64 * a + 64)
                    if p is not None:
                        pe.wait_ge(xT_sb, p + 1)
                    if at_start(a):
                        pe.wait_ge(act_setup, 1)
                        pe.wait_ge(own, 8)
                        pe.wait_ge(stack_pads, 1)
                elif b == 0 and g == 1:
                    pe.wait_ge(v_sb, a + 1)
                else:
                    pe.wait_ge(max_sb, n - 1)
                if g == 0:
                    mm(bank[:], dist16[:], slope_hi[:, 0:HG, :], start=True, stop=False, skip_group_check=True)
                for h in range(HG * g, HG * g + HG):
                    o = (h - HG * g) * P
                    last = mm(bank[:, o:o + P], qs[0:ZROWS, h, b * P:(b + 1) * P], ks[0:ZROWS, h, b * P:(b + 1) * P],
                              start=(g > 0), stop=True, skip_group_check=True)
                last.then_inc(s_mm, 1)

            def shift_T(a, b):
                pe.wait_ge(ns_sb, 2 * a + b + 1)
                if b == 1:
                    pe.wait_ge(nm_sb, 2 * a + 1)
                nc.tensor.transpose(ps_nm, nsplit[:, b, :, :].rearrange("p s h -> p (s h)"), ident16[:]).then_inc(nm_mm, 1)

            def scores_T(a, b, g, f=None, p=None):
                bank = ps_st[g % 2]
                if f is not None:
                    pe.wait_ge(lsh_sb, f + 1)
                if p is not None:
                    pe.wait_ge(qklo_sb, 2 * p + 2)
                if at_start(a) and b == 0:
                    if g >= 2:
                        pe.wait_ge(exp_sb, g - 1)
                else:
                    pe.wait_ge(exp_sb, 2 * NHG * a + NHG * b + g - 1)
                if g == 0:
                    pe.wait_ge(s_nm[b], 16 * a + 16)
                    if at_start(a):
                        pe.wait_ge(act_setup, 2)
                        pe.wait_ge(stack_pads, 2)
                h0, first = HG * g, True
                n_split = min(max(SPLIT_SLOPES - h0, 0), HG)
                n_small = min(max(SPLIT_SLOPES + SMALL_SLOPES - h0, 0), HG) - n_split
                if n_split:
                    for part in (slope_hi, slope_lo):
                        mm(bank[:, 0:n_split * P], dist16[:], part[:, h0:h0 + n_split, :], start=first, stop=False,
                           skip_group_check=True)
                        first = False
                if n_small:
                    j = h0 + n_split - SPLIT_SLOPES
                    mm(bank[:, n_split * P:(n_split + n_small) * P], dist16[:], slope_small[:, j:j + n_small, :],
                       start=first, stop=False, skip_group_check=True)
                    first = False
                for h in range(h0, h0 + HG):
                    o = (h - h0) * P
                    last = mm(bank[:, o:o + P], ks[:, h, b * P:(b + 1) * P], qs[:, h, b * P:(b + 1) * P],
                              start=first, stop=True, skip_group_check=True)
                    first = False
                last.then_inc(st_mm, 1)

            def weigh_values(a, b, f=None):
                pe.wait_ge(exp_sb, 2 * NHG * a + NHG * (b + 1))
                if b == 0:
                    pe.wait_ge(v_sb, a + 1)
                    pe.wait_ge(nm_sb, 2 * a + 2)
                if f is not None:
                    pe.wait_ge(cwT_sb, f + 1)
                if not (at_start(a) and b == 0):
                    pe.wait_ge(attn_sb, 2 * a + b)
                for r in range(2):
                    n = (3, 1)[r]
                    for c in range(4):
                        h = 3 * c if r == 0 else 12 + c
                        last = mm(ps_pv[32 * c:32 * c + 32, r * 3 * P:(r * 3 + n) * P], v_aug[:, b, r, c, :],
                                  probs[:, b, h * P:(h + n) * P], start=True, stop=True, skip_group_check=True)
                last.then_inc(pv_mm, 1)

            def values_T(a, b):
                pe.wait_ge(pvev_sb, 2 * a + b + 1)
                for l in range(4):
                    last = nc.tensor.transpose(ps_pv[:, l * P:(l + 1) * P], pv_sb[:, l * P:(l + 1) * P], ident[:])
                last.then_inc(pvT_mm, 1)

            def attention_T(a, b, f):
                pe.wait_ge(attn_sb, 2 * a + b + 1)
                if not (at_start(a) and b == 0):
                    pe.wait_ge(x1_sb, 2 * a + b)
                if f is not None and not at_start(f):
                    pe.wait_ge(y_sb, f)
                nc.tensor.transpose(ps_aT, attn[:], ident[:]).then_inc(aT_mm, 1)

            def project_out(a, b):
                pe.wait_ge(aT_sb, 2 * a + b + 1)
                mm(ps_o, attnT[:], wT[:, 3, :], start=True, stop=True).then_inc(o_mm, 1)

            def expert_in_T(f):
                pe.wait_ge(x2n_sb, NB * f + NB)
                for b in range(NB):
                    last = nc.tensor.transpose(ps_x2T[:, b * P:(b + 1) * P], x2n[:, b, :], ident[:])
                last.then_inc(x2T_mm, 1)

            def router(f):
                for b in range(NB):
                    for n, (u, w) in enumerate(((x2_lo, wr_hi), (x2_hi, wr_lo), (x2_hi, wr_hi))):
                        last = mm(ps_lg[:, b * E:(b + 1) * E], u[:, b * P:(b + 1) * P], w[:], start=(n == 0), stop=(n == 2))
                last.then_inc(lg_mm, 1)

            def weights_T(f, a):
                pe.wait_ge(cw_sb, f + 1)
                if a is not None:
                    pe.wait_ge(nm_sb, 2 * a + 2)
                for b in range(NB):
                    last = nc.tensor.transpose(ps_cwT[:, b * P:(b + 1) * P], cw[:, b, :], ident[:])
                last.then_inc(cwT_mm, 1)

            def up(f, c):
                if c == 0:
                    pe.wait_ge(x2hi_sb, f + 1)
                    if at_start(f):
                        pe.wait_ge(act_setup, 5)
                        pe.wait_ge(dve_setup, 5)
                if not (at_start(f) and c < 2):
                    pe.wait_ge(hid_sb, NCH * f + max(c - 1, 0))
                gate_up = ((wg_hi, wg_lo), (wu_hi, wu_lo))
                for k, weights in enumerate(gate_up):
                    for n, w in enumerate(weights):
                        mm(ps_up[c % 2][:, k, :], w[:, c, :], x2_hi[:], start=(k == 0 and n == 0), stop=False,
                           skip_group_check=True)
                if c == 0:
                    pe.wait_ge(x2lo_sb, f + 1)
                for k, (hi, _) in enumerate(gate_up):
                    last = mm(ps_up[c % 2][:, k, :], hi[:, c, :], x2_lo[:], start=False, stop=True, skip_group_check=True)
                last.then_inc(up_mm, 1)

            def down(f, chunks, out_product=None):
                for c in chunks:
                    if c == 0:
                        if at_start(f):
                            pe.wait_ge(pool_setup, 1)
                        elif out_product is None:
                            pe.wait_ge(y_sb, f)
                        if out_product is not None:
                            pe.wait_ge(x1_sb, 2 * out_product + 2)
                    if c == SHARED:
                        pe.wait_ge(hid_sb, NCH * f + NCH)
                    elif c % 2 == 0:
                        pe.wait_ge(hc_sb, PAIRS * f + c // 2 + 1)
                    for b in range(NB):
                        last = mm(ps_dn[:, b * P:(b + 1) * P], hid[:, c, b * P:(b + 1) * P], wd_sb[:, c, :],
                                  start=(c == 0 and b == 0), stop=(c == SHARED), skip_group_check=True)
                    last.then_inc(dn_mm, 1)

            def step(f, a, p, q):
                fs, as_, ps, qs_ = f is not None, a is not None, p is not None, q is not None

                def late_down(*chunks):
                    if fs and not at_start(f): down(f - 1, chunks, f)

                if as_: scores(a, 0, 0, p)
                if as_: scores(a, 0, 1)
                late_down(0)
                if ps:
                    project_q(p)
                    project_k(p)
                if as_: scores(a, 0, 2)
                if fs: expert_in_T(f)
                late_down(1)
                if as_: scores(a, 0, 3)
                if fs: up(f, 0)
                if as_: scores(a, 1, 0)
                if fs: up(f, 1)
                late_down(2)
                if as_:
                    scores(a, 1, 1)
                    shift_T(a, 0)
                if fs: router(f)
                late_down(3)
                if as_: scores(a, 1, 2)
                if fs: up(f, 2)
                late_down(4)
                if as_: scores(a, 1, 3)
                if fs: up(f, 3)
                late_down(5)
                if as_: scores_T(a, 0, 0, f=f)
                late_down(6)
                if as_:
                    shift_T(a, 1)
                    scores_T(a, 0, 1, p=p)
                late_down(7)
                if fs: up(f, 4)
                if as_: scores_T(a, 0, 2)
                late_down(8)
                if fs: weights_T(f, a)
                if as_: scores_T(a, 0, 3)
                if fs: up(f, 5)
                if as_:
                    scores_T(a, 1, 0)
                    weigh_values(a, 0, f)
                    scores_T(a, 1, 1)
                    values_T(a, 0)
                    scores_T(a, 1, 2)
                if fs: up(f, 6)
                if ps and not at_start(p):
                    pe.wait_ge(pairs_sb, 3 * p)
                if as_:
                    scores_T(a, 1, 3)
                    attention_T(a, 0, f)
                if qs_: project_x(q)
                if fs: up(f, 7)
                if as_:
                    weigh_values(a, 1)
                    project_out(a, 0)
                if ps: project_v(p)
                if as_: values_T(a, 1)
                if fs: up(f, 8)
                if as_:
                    attention_T(a, 1, f)
                    project_out(a, 1)

            step(None, None, None, 0)
            step(None, None, 0, 1)
            step(None, 0, 1, 2)
            run_steps(pe, step)
            f = NG - 1
            down(f - 1, (0, 1), f)
            expert_in_T(f)
            up(f, 0)
            router(f)
            down(f - 1, (2, 3))
            up(f, 1)
            up(f, 2)
            down(f - 1, (4, 5))
            weights_T(f, None)
            up(f, 3)
            down(f - 1, (6, 7, 8))
            up(f, 4)
            up(f, 5)
            up(f, 6)
            up(f, 7)
            down(f, (0, 1))
            up(f, 8)
            down(f, range(2, NCH))

        @block.scalar
        def _(act):
            fn = nc.scalar.activation

            def x_T(p):
                act.wait_ge(xT_mm, p + 1)
                fn(xnT[:], ps_xT, ACT.Copy).then_inc(xT_sb, 1)

            def qk_high(p):
                act.wait_ge(qk_mm, p + 1)
                if at_start(p):
                    act.wait_ge(dve_setup, 2)
                else:
                    act.wait_ge(s_stack, 64 * p)
                for k in range(2):
                    fn(qk_parts[:, 0, k, :], ps_qk[:, k * T:(k + 1) * T], ACT.Identity, bias=bqk_sb[:, k:k + 1]).then_inc(qkhi_sb, 1)

            def shift_copy(a, b):
                act.wait_ge(nm_mm, 2 * a + b + 1)
                if not at_start(a):
                    act.wait_ge(s_nm[b], 16 * a)
                fn(nmT[:, b, :], ps_nm, ACT.Copy).then_inc(nm_sb, 1)

            def exponential(a, b, g):
                act.wait_ge(st_mm, 2 * NHG * a + NHG * b + g + 1)
                if g == 0 and not at_start(a):
                    act.wait_ge(pv_mm, 2 * a + b - 1)
                fn(probs[:, b, g * HG * P:(g + 1) * HG * P], ps_st[g % 2][:], ACT.Exp).then_inc(exp_sb, 1)

            def values_copy(a, b):
                act.wait_ge(pv_mm, 2 * a + b + 1)
                if not (at_start(a) and b == 0):
                    act.wait_ge(pvT_mm, 2 * a + b)
                fn(pv_sb[:], ps_pv[:], ACT.Copy).then_inc(pvev_sb, 1)

            def attention_copy(a, b):
                act.wait_ge(aT_mm, 2 * a + b + 1)
                if not (at_start(a) and b == 0):
                    act.wait_ge(o_mm, 2 * a + b)
                fn(attnT[:], ps_aT, ACT.Copy).then_inc(aT_sb, 1)

            def x2_high(f):
                act.wait_ge(x2T_mm, f + 1)
                if not at_start(f):
                    act.wait_ge(up_mm, NCH * f)
                fn(x2_hi[:], ps_x2T, ACT.Copy).then_inc(x2hi_sb, 1)

            def router_exp(f):
                act.wait_ge(lsh_sb, f + 1)
                if not at_start(f):
                    act.wait_ge(route_sb, ROUTE * f)
                fn(le[:], lsh[:], ACT.Exp).then_inc(lexp_sb, 1)

            def weights_copy(f):
                act.wait_ge(cwT_mm, f + 1)
                if not at_start(f):
                    act.wait_ge(s_cwd, 16 * f)
                fn(cwT[:], ps_cwT, ACT.Copy).then_inc(cwT_sb, 1)

            def tanh(f, c):
                act.wait_ge(up_mm, NCH * f + c + 1)
                if not (at_start(f) and c < 2):
                    act.wait_ge(tg_sb, NCH * f + max(c - 1, 0))
                fn(th[:, c % 2, :], ps_up[c % 2][:, 0, :], ACT.Tanh, scale=0.5).then_inc(tanh_sb, 1)

            def step(f, a, p, q):
                fs, as_, ps, qs_ = f is not None, a is not None, p is not None, q is not None
                if fs: x2_high(f)
                if ps: qk_high(p)
                if fs:
                    tanh(f, 0)
                    tanh(f, 1)
                if as_: shift_copy(a, 0)
                if fs:
                    tanh(f, 2)
                    router_exp(f)
                    tanh(f, 3)
                if as_:
                    exponential(a, 0, 0)
                    shift_copy(a, 1)
                    exponential(a, 0, 1)
                if fs: tanh(f, 4)
                if as_: exponential(a, 0, 2)
                if fs: weights_copy(f)
                if as_: exponential(a, 0, 3)
                if fs: tanh(f, 5)
                if as_:
                    exponential(a, 1, 0)
                    values_copy(a, 0)
                    exponential(a, 1, 1)
                    exponential(a, 1, 2)
                    exponential(a, 1, 3)
                if fs: tanh(f, 6)
                if as_: attention_copy(a, 0)
                if qs_: x_T(q)
                if fs: tanh(f, 7)
                if as_:
                    values_copy(a, 1)
                    attention_copy(a, 1)
                if fs: tanh(f, 8)

            nc.scalar.preload_act_table(ACT.Exp)
            act.wait_ge(s_x, 16)
            act.wait_ge(s_ctx, 16)
            act.dma_start(x_all[:, 2 * NB:, :], x[:, 2 * NB:, :]).then_inc(s_x, 16)
            act.dma_start(ctx_all[:, 2 * T:], ctxT[:, 2 * T:]).then_inc(s_ctx, 16)
            act.dma_start(wg_sb[:], wgT).then_inc(s_wexp, 16)
            act.dma_start(wu_sb[:], wuT).then_inc(s_wexp, 16)
            act.dma_start(wr_sb[:], wr).then_inc(s_wexp, 16)
            act.dma_start(wd_sb[:], wd).then_inc(s_wexp, 16)
            act.wait_ge(s_const, 32)
            step(None, None, None, 0)
            for h in range(SPLIT_SLOPES):
                last = fn(slope_hi[:, h, :], ident[:], ACT.Copy, scale=float(m_hi[h]))
            last.then_inc(act_setup, 1)
            step(None, None, 0, 1)
            for h in range(SPLIT_SLOPES):
                fn(slope_lo[:, h, :], ident[:], ACT.Copy, scale=float(m_lo[h]))
            for j in range(SMALL_SLOPES):
                last = fn(slope_small[:, j, :], ident[:], ACT.Copy, scale=float(m[SPLIT_SLOPES + j]))
            last.then_inc(act_setup, 1)
            act.wait_ge(s_wexp, 64)
            fn(wg_hi[:], wg_sb[:], ACT.Copy).then_inc(act_setup, 1)
            fn(wu_hi[:], wu_sb[:], ACT.Copy).then_inc(act_setup, 1)
            fn(wr_hi[:], wr_sb[:], ACT.Copy).then_inc(act_setup, 1)
            step(None, 0, 1, 2)
            run_steps(act, step)
            f = NG - 1
            x2_high(f)
            tanh(f, 0)
            router_exp(f)
            tanh(f, 1)
            tanh(f, 2)
            weights_copy(f)
            for c in range(3, NCH):
                tanh(f, c)

        @block.vector
        def _(dve):
            v = nc.vector

            def carry_wait():
                v.memset(carrier[:], 0.0)

            def norm1_stats(p):
                if at_start(p):
                    dve.wait_ge(s_x, 16)
                elif isinstance(p, int) and p == 2:
                    dve.wait_ge(s_x, 32)
                for b in range(NB):
                    v.bn_stats(stats1[:, b, :], x_all[:, p * NB + b, :]).then_inc(st1_sb, 1)

            def norm1_mean(p):
                dve.wait_ge(st1_sb, NB * p + NB)
                if not at_start(p):
                    dve.wait_ge(ve1_sb, p)
                carry_wait()
                for b in range(NB):
                    v.bn_aggr(mv1[:, b, :], stats1[:, b, :]).then_inc(mv1_sb, 1)

            def norm1(p):
                dve.wait_ge(rstd1_sb, p + 1)
                dve.wait_ge(mv1_sb, NB * p + NB)
                if not at_start(p):
                    dve.wait_ge(xT_mm, p)
                for b in range(NB):
                    last = v.tensor_scalar(xn[:, b, :], x_all[:, p * NB + b, :], mv1[:, b, 0:1], rstd1[:, b:b + 1],
                                           ALU.subtract, ALU.mult)
                last.then_inc(xn_sb, 1)

            def qk_low(p, k):
                dve.wait_ge(qkhi_sb, 2 * p + 2)
                if not at_start(p):
                    dve.wait_ge(s_stack, 64 * p)
                v.scalar_tensor_tensor(out=qk_parts[:, 1, k, :], in0=ps_qk[:, k * T:(k + 1) * T], scalar=bqk_sb[:, k:k + 1],
                                       in1=qk_parts[:, 0, k, :], op0=ALU.add, op1=ALU.subtract).then_inc(qklo_sb, 1)

            def pair_first_parts():
                dve.wait_ge(qklo_sb, 2)
                v.tensor_copy(qk_parts[:, 2:4, 1, :], qk_parts[:, 0:2, 1, :]).then_inc(first_pairs, 1)
                for i in range(2):
                    v.tensor_copy(qk_parts[:, 2 + i, 0, :], qk_parts[:, 1 - i, 0, :]).then_inc(first_pairs, 1)

            def values(p):
                dve.wait_ge(v_mm, p + 1)
                if at_start(p):
                    dve.wait_ge(s_small, 32)
                else:
                    dve.wait_ge(pv_mm, 2 * p)
                for b in range(NB):
                    for r, (h0, n) in enumerate(((0, 3), (12, 1))):
                        w = n * DH
                        src = ps_v[:, b * P + h0 * DH:b * P + h0 * DH + 4 * w].rearrange("p (c w) -> p c w", c=4)
                        bias = bv_rep[:, h0 * DH:h0 * DH + 4 * w].rearrange("p (c w) -> p c w", c=4)
                        last = v.tensor_tensor(v_aug[:, b, r, :, 0:w], src, bias, ALU.add)
                last.then_inc(v_sb, 1)

            def row_max(a, b, g):
                dve.wait_ge(s_mm, 2 * NHG * a + NHG * b + g + 1)
                v.tensor_reduce(nmax[:, b, HG * g:HG * g + HG], ps_s[g % 2][:].rearrange("p (h j) -> p h j", h=HG), AX_X, ALU.max,
                                negate=True).then_inc(max_sb, 1)

            def max_high(a, b):
                dve.wait_ge(max_sb, 2 * NHG * a + NHG * (b + 1))
                v.tensor_copy(nsplit[:, b, 0, :], nmax[:, b, :]).then_inc(nh_sb, 1)

            def max_low(a, b):
                dve.wait_ge(nh_sb, 2 * a + b + 1)
                v.tensor_tensor(nsplit[:, b, 1, :], nmax[:, b, :], nsplit[:, b, 0, :], ALU.subtract).then_inc(ns_sb, 1)

            def row_sums(a, b):
                dve.wait_ge(pvT_mm, 2 * a + b + 1)
                row = ps_pv[:].ap[0]
                v.reciprocal(rden[:], bass.AP(ps_pv, 24, [list(row), [P, 4], [32, 4]])).then_inc(rden_sb, 1)

            def normalise(a, b):
                row = ps_pv[:].ap[0]
                dve.wait_ge(rden_sb, 2 * a + b + 1)
                if not (at_start(a) and b == 0):
                    dve.wait_ge(aT_mm, 2 * a + b)
                v.tensor_tensor(attn[:, 0:96].rearrange("p (c l d) -> p l c d", c=4, l=3),
                                bass.AP(ps_pv, 0, [list(row), [P + DH, 3], [32, 4], [1, DH]]),
                                rden[:, 0:3, :].unsqueeze(3).to_broadcast([P, 3, 4, DH]), ALU.mult)
                v.tensor_tensor(attn[:, 96:128].rearrange("p (c d) -> p c d", c=4),
                                bass.AP(ps_pv, 3 * P, [list(row), [32, 4], [1, DH]]),
                                rden[:, 3, :].unsqueeze(2).to_broadcast([P, 4, DH]), ALU.mult).then_inc(attn_sb, 1)

            def residual1(a, b):
                dve.wait_ge(o_mm, 2 * a + b + 1)
                dve.wait_ge(xb_sb, a + 1)
                v.tensor_tensor(x1_all[:, a * NB + b, :], ps_o, xb[:, b, :], ALU.add).then_inc(x1_sb, 1)

            def norm2_stats(a, b):
                dve.wait_ge(x1_sb, 2 * a + b + 1)
                carry_wait()
                v.bn_stats(stats2[:, b, :], x1_all[:, a * NB + b, :]).then_inc(st2_sb, 1)

            def norm2_mean(a, b):
                dve.wait_ge(st2_sb, 2 * a + b + 1)
                if not at_start(a):
                    dve.wait_ge(ve2_sb, 2 * a + b - 1)
                carry_wait()
                v.bn_aggr(mv2[:, b, :], stats2[:, b, :]).then_inc(mv2_sb, 1)

            def norm2(a, b):
                dve.wait_ge(rstd2_sb, 2 * a + b + 1)
                dve.wait_ge(mv2_sb, 2 * a + b + 1)
                if not at_start(a):
                    dve.wait_ge(x2T_mm, a)
                v.tensor_scalar(x2n[:, b, :], x1_all[:, a * NB + b, :], mv2[:, b, 0:1], rstd2[:, b:b + 1],
                                ALU.subtract, ALU.mult).then_inc(x2n_sb, 1)

            def x2_low(f):
                dve.wait_ge(x2hi_sb, f + 1)
                if not at_start(f):
                    dve.wait_ge(up_mm, NCH * f)
                v.tensor_tensor(x2_lo[:], ps_x2T, x2_hi[:].bitcast(F32), ALU.subtract).then_inc(x2lo_sb, 1)

            logits = ps_lg.rearrange("p (b e) -> p b e", b=NB)

            def router_max(f):
                dve.wait_ge(lg_mm, f + 1)
                v.tensor_reduce(lmax[:], logits, AX_X, ALU.max).then_inc(lmax_sb, 1)

            def router_shift(f):
                if not at_start(f):
                    dve.wait_ge(lexp_sb, f)
                dve.wait_ge(lmax_sb, f + 1)
                v.tensor_tensor(lsh[:], logits, lmax[:].unsqueeze(2).to_broadcast([P, NB, E]), ALU.subtract).then_inc(lsh_sb, 1)

            def route(f, i):
                if i == 0:
                    dve.wait_ge(lexp_sb, f + 1)
                else:
                    dve.wait_ge(route_sb, ROUTE * f + i)
                if i == 0:
                    last = v.tensor_reduce(lsum[:], le[:], AX_X, ALU.add)
                elif i == 1:
                    last = v.reciprocal(lrec[:], lsum[:])
                elif i == 2:
                    last = v.tensor_tensor(pr[:, :, 0:E], le[:], lrec[:].unsqueeze(2).to_broadcast([P, NB, E]), ALU.mult)
                elif i == 3:
                    carry_wait()
                    for b in range(NB):
                        last = v.max(top8[:, b, :], pr[:, b, 0:E])
                elif i == 4:
                    last = v.tensor_copy(drop8[:, :, 0:2], top8[:, :, 0:2])
                elif i == 5:
                    carry_wait()
                    for b in range(NB):
                        last = v.match_replace(rest[:, b, :], drop8[:, b, :], pr[:, b, :], 0.0)
                else:
                    if not at_start(f):
                        dve.wait_ge(cwT_mm, f)
                    v.tensor_tensor(cw[:], pr[:, :, 0:E], rest[:, :, 0:E], ALU.subtract).then_inc(cw_sb, 1)
                    return
                last.then_inc(route_sb, 1)

            def gate(f, c):
                dve.wait_ge(tanh_sb, NCH * f + c + 1)
                v.scalar_tensor_tensor(out=tg[:, c % 2, :], in0=th[:, c % 2, :], scalar=1.0, in1=ps_up[c % 2][:, 0, :],
                                       op0=ALU.add, op1=ALU.mult).then_inc(tg_sb, 1)

            def hidden(f, c):
                dve.wait_ge(tg_sb, NCH * f + c + 1)
                v.tensor_tensor(hid[:, c, :], tg[:, c % 2, :], ps_up[c % 2][:, 1, :], ALU.mult).then_inc(hid_sb, 1)

            def residual2(f):
                dve.wait_ge(dn_mm, NCH * f + NCH)
                x1 = x1_all[:, bass.ds(f * NB, NB), :]
                v.tensor_tensor(x1, ps_dn.rearrange("p (b d) -> p b d", b=NB), x1, ALU.add).then_inc(y_sb, 1)

            def step(f, a, p, q):
                fs, as_, ps, qs_ = f is not None, a is not None, p is not None, q is not None
                late = fs and not at_start(f)
                if as_: row_max(a, 0, 0)
                if late: gate(f - 1, 8)
                if fs: norm2(f, 1)
                if late: hidden(f - 1, 8)
                if as_:
                    row_max(a, 0, 1)
                    row_max(a, 0, 2)
                if fs: x2_low(f)
                if as_:
                    row_max(a, 0, 3)
                    max_high(a, 0)
                if fs: gate(f, 0)
                if as_: max_low(a, 0)
                if fs: hidden(f, 0)
                if as_: row_max(a, 1, 0)
                if fs: gate(f, 1)
                if as_: row_max(a, 1, 1)
                if fs:
                    hidden(f, 1)
                    router_max(f)
                if as_: row_max(a, 1, 2)
                if fs: router_shift(f)
                if ps: qk_low(p, 0)
                if fs: gate(f, 2)
                if ps:
                    qk_low(p, 1)
                    if at_start(p): pair_first_parts()
                if fs: hidden(f, 2)
                if as_: row_max(a, 1, 3)
                if fs: route(f, 0)
                if as_: max_high(a, 1)
                if fs: route(f, 1)
                if as_: max_low(a, 1)
                if fs:
                    route(f, 2)
                    gate(f, 3)
                    route(f, 3)
                    hidden(f, 3)
                    route(f, 4)
                if qs_: norm1_stats(q)
                if fs:
                    route(f, 5)
                    route(f, 6)
                    gate(f, 4)
                if qs_: norm1_mean(q)
                if fs:
                    hidden(f, 4)
                    if late: residual2(f - 1)
                    gate(f, 5)
                if qs_: norm1(q)
                if fs: hidden(f, 5)
                if as_:
                    row_sums(a, 0)
                    normalise(a, 0)
                if fs:
                    gate(f, 6)
                    hidden(f, 6)
                if fs: gate(f, 7)
                if as_: residual1(a, 0)
                if fs: hidden(f, 7)
                if as_:
                    norm2_stats(a, 0)
                    row_sums(a, 1)
                    norm2_mean(a, 0)
                    normalise(a, 1)
                if ps: values(p)
                if as_:
                    norm2(a, 0)
                    residual1(a, 1)
                    norm2_stats(a, 1)
                    norm2_mean(a, 1)

            v.memset(stacks_sb[2 * SROWS:ZROWS].bitcast(F32), 0.0).then_inc(stack_pads, 1)
            dve.wait_ge(s_wqkvo, 32)
            v.tensor_scalar(wT[:, 0, :], wT[:, 0, :], q_scale, None, ALU.mult).then_inc(dve_setup, 1)
            v.tensor_scalar(bqk_sb[:, 0:1], bqk_sb[:, 0:1], q_scale, None, ALU.mult).then_inc(dve_setup, 1)
            step(None, None, None, 0)
            step(None, None, 0, 1)
            v.memset(ks[ZROWS:AROWS].bitcast(F32), two_ones).then_inc(stack_pads, 1)
            step(None, 0, 1, 2)
            dve.wait_ge(act_setup, 5)
            v.tensor_tensor(wg_lo[:], wg_sb[:], wg_hi[:].bitcast(F32), ALU.subtract).then_inc(dve_setup, 1)
            v.tensor_tensor(wu_lo[:], wu_sb[:], wu_hi[:].bitcast(F32), ALU.subtract).then_inc(dve_setup, 1)
            v.tensor_tensor(wr_lo[:], wr_sb[:], wr_hi[:].bitcast(F32), ALU.subtract).then_inc(dve_setup, 1)
            run_steps(dve, step)
            f = NG - 1
            gate(f - 1, 8)
            hidden(f - 1, 8)
            norm2(f, 1)
            x2_low(f)
            gate(f, 0)
            router_max(f)
            hidden(f, 0)
            router_shift(f)
            gate(f, 1)
            hidden(f, 1)
            for i in range(ROUTE + 1):
                route(f, i)
            for c in range(2, NCH):
                gate(f, c)
                hidden(f, c)
                if c == 4: residual2(f - 1)
            residual2(f)

        @block.gpsimd
        def _(pool):
            g = nc.gpsimd

            def carry_wait(place):
                g.tensor_tensor(pool_carrier[:, place:place + 1], neg_half[:, 0:1], neg_half[:, 0:1], ALU.add)

            def inverse_deviation1(q):
                pool.wait_ge(mv1_sb, NB * q + NB)
                g.tensor_tensor(ve1[:], mv1[:, :, 1], eps_sb[:], ALU.add).then_inc(ve1_sb, 1)
                pool.wait_ge(ve1_sb, q + 1)
                if not at_start(q):
                    pool.wait_ge(xn_sb, q)
                g.tensor_tensor(rstd1[:], ve1[:], neg_half[:], ALU.pow).then_inc(rstd1_sb, 1)

            def inverse_deviation2(a, b):
                pool.wait_ge(mv2_sb, 2 * a + b + 1)
                g.tensor_tensor(ve2[:, b:b + 1], mv2[:, b, 1:2], eps_sb[:, b:b + 1], ALU.add).then_inc(ve2_sb, 1)
                pool.wait_ge(ve2_sb, 2 * a + b + 1)
                if not at_start(a):
                    pool.wait_ge(x2n_sb, 2 * a + b - 1)
                g.tensor_tensor(rstd2[:, b:b + 1], ve2[:, b:b + 1], neg_half[:, b:b + 1], ALU.pow).then_inc(rstd2_sb, 1)

            def add_bo(a):
                if at_start(a):
                    pool.wait_ge(s_small, 32)
                    pool.wait_ge(s_x, 16)
                else:
                    if isinstance(a, int) and a == 2:
                        pool.wait_ge(s_x, 32)
                    pool.wait_ge(x1_sb, 2 * a)
                for b in range(NB):
                    last = g.tensor_tensor(xb[:, b, :], x_all[:, a * NB + b, :], bo_rep[:], ALU.add)
                last.then_inc(xb_sb, 1)

            def copy_ctx(p):
                if at_start(p):
                    pool.wait_ge(s_ctx, 16)
                else:
                    if isinstance(p, int) and p == 2:
                        pool.wait_ge(s_ctx, 32)
                    pool.wait_ge(v_mm, p)
                carry_wait(0)
                g.tensor_copy(ctx_g[:], ctx_all[:, bass.ds(p * T, T)]).then_inc(ctx_sb, 1)

            def pair_parts(p):
                pool.wait_ge(qkhi_sb, 2 * p + 2)
                pool.wait_ge(qklo_sb, 2 * p + 2)
                pool.wait_ge(s_stack, 64 * p)
                carry_wait(1)
                g.tensor_copy(qk_parts[:, 2:4, 1, :], qk_parts[:, 0:2, 1, :]).then_inc(pairs_sb, 1)
                for i in range(2):
                    g.tensor_copy(qk_parts[:, 2 + i, 0, :], qk_parts[:, 1 - i, 0, :]).then_inc(pairs_sb, 1)

            def weigh_experts(f, pair):
                if pair == 0:
                    pool.wait_ge(s_crep, 32 * f + 32)
                pool.wait_ge(hid_sb, NCH * f + 2 * pair + 2)
                h2, c2 = hid[:, 2 * pair:2 * pair + 2, :], crep[:, 2 * pair:2 * pair + 2, :]
                g.tensor_tensor(h2, h2, c2, ALU.mult).then_inc(hc_sb, 1)

            def step(f, a, p, q):
                if f is not None and not at_start(f):
                    for pair in range(1, PAIRS):
                        weigh_experts(f - 1, pair)
                if p is not None and not at_start(p):
                    pair_parts(p)
                if q is not None:
                    inverse_deviation1(q)
                if a is not None:
                    add_bo(a)
                if p is not None:
                    copy_ctx(p)
                if a is not None:
                    inverse_deviation2(a, 0)
                if f is not None:
                    weigh_experts(f, 0)
                if a is not None:
                    inverse_deviation2(a, 1)

            g.memset(neg_half[:], -0.5).then_inc(own, 1)
            g.memset(eps_sb[:], EPS).then_inc(own, 1)
            g.memset(v_aug[:], 1.0).then_inc(own, 1)
            g.memset(pr[:, :, E:], -1.0).then_inc(own, 1)
            g.memset(drop8[:], -1.0).then_inc(own, 1)
            pool.wait_ge(own, 5)
            g.memset(v_aug[:, :, 1, :, DH:3 * DH], 0.0).then_inc(own, 1)
            pool.wait_ge(own, 6)
            g.memset(stacks_sb[SROWS:2 * SROWS].bitcast(F32), 0.0).then_inc(own, 1)
            pool.wait_ge(own, 7)
            step(None, None, None, 0)
            pool.wait_ge(s_const, 32)
            pool.wait_ge(rstd1_sb, 1)
            g.tensor_copy(ident16[:], ident[:]).then_inc(own, 1)
            pool.wait_ge(own, 8)
            step(None, None, 0, 1)
            step(None, 0, 1, 2)
            pool.wait_ge(rstd2_sb, 2)
            pool.wait_ge(s_wexp, 64)
            g.tensor_scalar(wd_sb[:], wd_sb[:], 0.5, None, ALU.mult).then_inc(pool_setup, 1)
            pool.wait_ge(pool_setup, 1)
            run_steps(pool, step)
            for pair in range(1, PAIRS):
                weigh_experts(NG - 2, pair)
            for pair in range(PAIRS):
                weigh_experts(NG - 1, pair)


def kernel(x, ctx_1024, L0_xattn_Wq, L0_xattn_bq, L0_xattn_Wk, L0_xattn_bk, L0_xattn_Wv, L0_xattn_bv, L0_xattn_Wo,
           L0_xattn_bo, L0_ffn_Wr, L0_ffn_Wg, L0_ffn_Wu, L0_ffn_Wd, L0_ffn_Sg, L0_ffn_Su, L0_ffn_Sd):
    import numpy as np
    import concourse.bacc as bacc
    from concourse.bass_utils import run_bass_kernel_spmd

    def rows(a):
        return np.ascontiguousarray(a)

    def by_dim(w):
        return np.asarray(w).reshape(H, DH, -1).transpose(2, 1, 0).reshape(P, P)

    x, ctx = np.asarray(x), np.asarray(ctx_1024)
    B = x.shape[0]
    arrays = {
        "x": rows(x.transpose(1, 0, 2)),
        "ctxT": rows(ctx.transpose(2, 0, 1).reshape(P, B * P)),
        "wqkvoT": rows(np.stack([by_dim(L0_xattn_Wq), by_dim(L0_xattn_Wk), np.asarray(L0_xattn_Wv).T,
                                 np.asarray(L0_xattn_Wo).T], axis=1)),
        "bqk": rows(np.stack([np.asarray(b).reshape(H, DH).T.reshape(P) for b in (L0_xattn_bq, L0_xattn_bk)], axis=1)),
        "bv": rows(L0_xattn_bv), "bo": rows(L0_xattn_bo),
        "wgT": rows(np.concatenate([np.asarray(L0_ffn_Wg).transpose(1, 0, 2).reshape(P, E * FE), np.asarray(L0_ffn_Sg)],
                                   axis=1).reshape(P, NCH, P)),
        "wuT": rows(np.concatenate([np.asarray(L0_ffn_Wu).transpose(1, 0, 2).reshape(P, E * FE), np.asarray(L0_ffn_Su)],
                                   axis=1).reshape(P, NCH, P)),
        "wd": rows(np.concatenate([np.asarray(L0_ffn_Wd).reshape(E * FE, P), np.asarray(L0_ffn_Sd)],
                                  axis=0).reshape(NCH, P, P).transpose(1, 0, 2)),
        "wr": rows(L0_ffn_Wr),
        **constants(),
    }
    nc = bacc.Bacc("TRN2", target_bir_lowering=False, num_devices=1)
    aps = {n: nc.dram_tensor(f"in_{n}", a.shape, mybir.dt.from_np(a.dtype), kind="ExternalInput").ap()
           for n, a in arrays.items()}
    out = nc.dram_tensor("out_y", (P, B, P), F32, kind="ExternalOutput").ap()
    xattn_moe_kernel(nc, out=out, **aps)
    r = run_bass_kernel_spmd(nc, [{f"in_{n}": a for n, a in arrays.items()}], core_ids=[0])
    return r.results[0]["out_y"].transpose(1, 0, 2)
```

```python
from contextlib import ExitStack

import numpy as np
import concourse.bass as bass
from concourse import mybir

F32 = mybir.dt.float32
F32R = mybir.dt.float32r
F16 = mybir.dt.float16
BF16 = mybir.dt.bfloat16
ALU = mybir.AluOpType
ACT = mybir.ActivationFunctionType
AX_X = mybir.AxisListType.X

P = 128
H, DH = 16, 8
HG = 4
NHG = H // HG
NB = 2
T = NB * P
E, FE = 16, 64
NCH = E * FE // P + 1
SHARED = NCH - 1
PAIRS = SHARED // 2
EPS = 1e-5
BIAS_A = 1000.0
BIAS_SCALE = 16384.0
SPLIT_SLOPES = 7
SMALL_SLOPES = 4
SROWS = 4 * DH
ZROWS = 96
AROWS = ZROWS + 2


def at_start(i):
    return isinstance(i, int) and i == 0


def slopes():
    hh = np.arange(1, H + 1, dtype=np.float32)
    return np.exp(-np.power(np.float32(5000.0), (hh - 1) / (H - 1) * np.float32(0.8))).astype(np.float32)


def constants():
    i = np.arange(P)
    dist = ((BIAS_A + np.abs(i[:, None] - i[None, :])) / BIAS_SCALE).astype(np.float16)
    feature = np.arange(E * FE).reshape(SHARED, P)
    select = (np.arange(E)[:, None, None] == feature[None] // FE).astype(np.float32)
    return {"c_ident": np.eye(P, dtype=np.float32), "c_dist": dist, "c_select": select}


def xattn_moe_kernel(nc, x, ctxT, wqkvoT, bqk, bv, bo, wgT, wuT, wd, wr, c_ident, c_dist, c_select, out):
    NG = x.shape[1] // NB
    m = slopes().astype(np.float64) * BIAS_SCALE
    m_hi = m.astype(np.float16)
    m_lo = (m - m_hi.astype(np.float64)).astype(np.float16)
    two_ones = float(np.array([1, 1], np.float16).view(np.float32)[0])
    q_scale = float(1.0 / np.sqrt(np.float32(DH)))

    stack = ExitStack()
    with stack:
        def sb(name, shape, dt=F32):
            return stack.enter_context(nc.sbuf_tensor(name, shape, dt))

        def psum(name, shape):
            return stack.enter_context(nc.psum_tensor(name, shape, F32))

        def sem(name):
            return stack.enter_context(nc.semaphore(name))

        x_all = sb("x_all", [P, NG * NB, P])
        x1_all = sb("x1_all", [P, NG * NB, P])
        wT = sb("wT", [P, 4, P])
        bqk_sb = sb("bqk_sb", [P, 2])
        bv_rep, bo_rep = sb("bv_rep", [P, P]), sb("bo_rep", [P, P])
        wg_sb, wu_sb, wd_sb = sb("wg_sb", [P, NCH, P]), sb("wu_sb", [P, NCH, P]), sb("wd_sb", [P, NCH, P])
        wr_sb = sb("wr_sb", [P, E])
        wg_hi, wg_lo = sb("wg_hi", [P, NCH, P], F32R), sb("wg_lo", [P, NCH, P], F32R)
        wu_hi, wu_lo = sb("wu_hi", [P, NCH, P], F32R), sb("wu_lo", [P, NCH, P], F32R)
        wr_hi, wr_lo = sb("wr_hi", [P, E], F32R), sb("wr_lo", [P, E], F32R)
        ident, ident16 = sb("ident", [P, P]), sb("ident16", [P, P], F16)
        dist16 = sb("dist16", [P, P], F16)
        select = sb("select", [E, SHARED, P])
        slope_hi = sb("slope_hi", [P, SPLIT_SLOPES, P], F16)
        slope_lo = sb("slope_lo", [P, SPLIT_SLOPES, P], F16)
        slope_small = sb("slope_small", [P, SMALL_SLOPES, P], BF16)
        neg_half, eps_sb = sb("neg_half", [P, NB]), sb("eps_sb", [P, NB])
        ctx_all = sb("ctx_all", [P, NG * T])
        ctx_g = sb("ctx_g", [P, T])
        stats1, mv1 = sb("stats1", [P, NB, 6]), sb("mv1", [P, NB, 2])
        ve1, rstd1 = sb("ve1", [P, NB]), sb("rstd1", [P, NB])
        xn, xnT = sb("xn", [P, NB, P]), sb("xnT", [P, T])
        qk_parts = sb("qk_parts", [P, 4, 2, T], F16)
        stacks_sb = sb("stacks_sb", [AROWS, H, 2, T], F16)
        qs, ks = stacks_sb[:, :, 0], stacks_sb[:, :, 1]
        v_aug = sb("v_aug", [P, NB, 2, 4, 32])
        nmax = sb("nmax", [P, NB, H])
        nsplit = sb("nsplit", [P, NB, 2, H], F16)
        nmT = sb("nmT", [2 * H, NB, P], F16)
        probs = sb("probs", [P, NB, H * P])
        pv_sb = sb("pv_sb", [P, 4 * P])
        rden = sb("rden", [P, 4, 4])
        attn, attnT = sb("attn", [P, P]), sb("attnT", [P, P])
        xb = sb("xb", [P, NB, P])
        stats2, mv2 = sb("stats2", [P, NB, 6]), sb("mv2", [P, NB, 2])
        ve2, rstd2 = sb("ve2", [P, NB]), sb("rstd2", [P, NB])
        x2n = sb("x2n", [P, NB, P])
        x2_hi, x2_lo = sb("x2_hi", [P, T], F32R), sb("x2_lo", [P, T], F32R)
        lmax, lsh, le = sb("lmax", [P, NB]), sb("lsh", [P, NB, E]), sb("le", [P, NB, E])
        lsum, lrec = sb("lsum", [P, NB]), sb("lrec", [P, NB])
        pr = sb("pr", [P, NB, E + 8])
        top8, drop8 = sb("top8", [P, NB, 8]), sb("drop8", [P, NB, 8])
        rest = sb("rest", [P, NB, E + 8])
        cw = sb("cw", [P, NB, E])
        cwT = sb("cwT", [E, T])
        select_r = sb("select_r", [E, SHARED, P], F32R)
        cwT_hi, cwT_lo = sb("cwT_hi", [E, T], F32R), sb("cwT_lo", [E, T], F32R)
        crep = sb("crep", [P, NCH - 1, T])
        th, tg = sb("th", [P, 2, T]), sb("tg", [P, 2, T])
        hid = sb("hid", [P, NCH, T])
        carrier, pool_carrier = sb("carrier", [P, 1]), sb("pool_carrier", [P, 2])
        cw_dram = nc.dram_tensor("cw_dram", [NG, E, T], F32, kind="Internal").ap()

        ps_s = [psum("ps_s0", [P, 512]), psum("ps_s1", [P, 512])]
        ps_st = [psum("ps_st0", [P, 512]), psum("ps_st1", [P, 512])]
        ps_pv = psum("ps_pv", [P, 512])
        ps_up = [psum("ps_up0", [P, 2, T]), psum("ps_up1", [P, 2, T])]
        ps_m = psum("ps_m", [P, 512])
        ps_nm = ps_pv[0:2 * H, T:T + P // 2].bitcast(F16)
        ps_qk, ps_v = ps_st[1], ps_s[1][:, 0:T]
        ps_x2T, ps_lg, ps_cwT = ps_st[0][:, 0:T], ps_st[0][:, T:T + NB * E], ps_pv[0:E, 0:T]
        ps_xT = ps_st[0][:, T:2 * T]
        ps_dn, ps_aT, ps_o = ps_m[:, 0:T], ps_m[:, T:T + P], ps_m[:, T + P:2 * T]
        ps_spread = [bank[:, i * T:(i + 1) * T] for bank in (ps_s[0], ps_s[1], ps_st[1], ps_st[0]) for i in range(2)]

        s_x, s_wqkvo, s_small, s_ident, s_dist, s_wg, s_wu, s_wd, s_x_rest, s_ctx_rest = (
            sem(n) for n in ("s_x", "s_wqkvo", "s_small", "s_ident", "s_dist", "s_wg", "s_wu", "s_wd", "s_x_rest",
                             "s_ctx_rest"))
        s_ctx, s_stack, s_cwd, s_crep, s_out = (sem(n) for n in ("s_ctx", "s_stack", "s_cwd", "s_crep", "s_out"))
        s_nm = [sem("s_nm0"), sem("s_nm1")]
        pool_setup, dve_setup, act_setup = sem("pool_setup"), sem("dve_setup"), sem("act_setup")
        xT_mm, qk_mm, v_mm, s_mm, nm_mm, st_mm, pv_mm, pvT_mm, aT_mm, o_mm, x2T_mm, lg_mm, cwT_mm, up_mm, dn_mm = (
            sem(n) for n in ("xT_mm", "qk_mm", "v_mm", "s_mm", "nm_mm", "st_mm", "pv_mm", "pvT_mm", "aT_mm", "o_mm",
                             "x2T_mm", "lg_mm", "cwT_mm", "up_mm", "dn_mm"))
        xT_sb, qkhi_sb, nm_sb, exp_sb, pvev_sb, aT_sb, x2hi_sb, lexp_sb, cwT_sb, tanh_sb = (
            sem(n) for n in ("xT_sb", "qkhi_sb", "nm_sb", "exp_sb", "pvev_sb", "aT_sb", "x2hi_sb", "lexp_sb", "cwT_sb",
                             "tanh_sb"))
        st1_sb, mv1_sb, xn_sb, qklo_sb, v_sb, max_sb, nh_sb, ns_sb, rden_sb, attn_sb, x1_sb, st2_sb, mv2_sb, x2n_sb = (
            sem(n) for n in ("st1_sb", "mv1_sb", "xn_sb", "qklo_sb", "v_sb", "max_sb", "nh_sb", "ns_sb", "rden_sb",
                             "attn_sb", "x1_sb", "st2_sb", "mv2_sb", "x2n_sb"))
        x2lo_sb, lmax_sb, lsh_sb, route_sb, cw_sb, tg_sb, hid_sb, y_sb = (
            sem(n) for n in ("x2lo_sb", "lmax_sb", "lsh_sb", "route_sb", "cw_sb", "tg_sb", "hid_sb", "y_sb"))
        ve1_sb, rstd1_sb, xb_sb, ve2_sb, rstd2_sb, hc_sb, pairs_sb, ctx_sb = (
            sem(n) for n in ("ve1_sb", "rstd1_sb", "xb_sb", "ve2_sb", "rstd2_sb", "hc_sb", "pairs_sb", "ctx_sb"))
        own = sem("pool_own")
        s_select, select_sb, cwTlo_sb, spread_mm, hw_sb = (
            sem(n) for n in ("s_select", "select_sb", "cwTlo_sb", "spread_mm", "hw_sb"))
        first_pairs = sem("first_pairs")
        stack_pads = sem("stack_pads")
        ROUTE = 6

        def run_steps(eng, step):
            step(0, 1, 2, 3)
            with eng.Fori(0, (NG - 4) // 2) as turn:
                for k in range(1, 3):
                    step(*(turn * 2 + (k + i) for i in range(4)))
            step(NG - 3, NG - 2, NG - 1, None)
            step(NG - 2, NG - 1, None, None)

        block = stack.enter_context(nc.Block())

        @block.sync
        def _(sp):
            def stacks(p):
                if not at_start(p):
                    sp.wait_ge(st_mm, 2 * NHG * p)
                for t in range(4):
                    if at_start(p):
                        sp.wait_ge((qkhi_sb, qklo_sb, first_pairs, first_pairs)[t], (2, 2, 2, 3)[t])
                    sp.dma_start(stacks_sb[DH * t:DH * (t + 1)].rearrange("d h k t -> d h (k t)"),
                                 qk_parts[:, t].rearrange("p k t -> p (k t)")).then_inc(s_stack, 16)

            def shift_rows(a, b):
                sp.wait_ge(nm_sb, 2 * a + b + 1)
                sp.dma_start(qs[ZROWS:AROWS, :, b * P:(b + 1) * P], nmT[:, b, :]).then_inc(s_nm[b], 16)

            def spread_weights(f):
                if not at_start(f):
                    sp.wait_ge(hc_sb, PAIRS * f)
                sp.wait_ge(cwT_sb, f + 1)
                sp.dma_start(cw_dram[f], cwT[:]).then_inc(s_cwd, 16)
                sp.wait_ge(s_cwd, 16 * f + 16)
                for odd in range(2):
                    src = bass.AP(cw_dram.tensor, f * (E * T) + odd * T, [[0, FE], [2 * T, E // 2], [1, T]])
                    sp.dma_start(crep[FE * odd:FE * (odd + 1), :, :], src).then_inc(s_crep, 16)

            def store(f):
                sp.wait_ge(y_sb, f + 1)
                sp.dma_start(out[:, bass.ds(f * NB, NB), :], x1_all[:, bass.ds(f * NB, NB), :]).then_inc(s_out, 16)

            def load_more():
                sp.wait_ge(s_nm[0], 16)
                sp.wait_ge(s_nm[1], 16)
                sp.dma_start(x_all[:, 2 * NB:4 * NB, :], x[:, 2 * NB:4 * NB, :]).then_inc(s_x, 16)
                sp.dma_start(ctx_all[:, 2 * T:4 * T], ctxT[:, 2 * T:4 * T]).then_inc(s_ctx, 16)

            def load_rest():
                sp.wait_ge(s_stack, 128)
                sp.dma_start(wd_sb[:], wd).then_inc(s_wd, 16)
                sp.dma_start(ctx_all[:, 4 * T:], ctxT[:, 4 * T:]).then_inc(s_ctx_rest, 16)
                sp.dma_start(x_all[:, 4 * NB:, :], x[:, 4 * NB:, :]).then_inc(s_x_rest, 16)
                sp.dma_start(select[:], c_select).then_inc(s_select, 16)

            def step(f, a, p, q):
                if a is not None:
                    shift_rows(a, 0)
                    shift_rows(a, 1)
                    if at_start(a): load_more()
                if f is not None:
                    spread_weights(f)
                if f is not None and not at_start(f):
                    store(f - 1)
                if p is not None:
                    stacks(p)

            sp.dma_start(x_all[:, 0:2 * NB, :], x[:, 0:2 * NB, :]).then_inc(s_x, 16)
            sp.dma_start(ident[:], c_ident).then_inc(s_ident, 16)
            sp.dma_start(wT[:], wqkvoT).then_inc(s_wqkvo, 16)
            sp.dma_start(bqk_sb[:], bqk).then_inc(s_wqkvo, 16)
            sp.dma_start(ctx_all[:, 0:2 * T], ctxT[:, 0:2 * T]).then_inc(s_ctx, 16)
            sp.dma_start(dist16[:], c_dist).then_inc(s_dist, 16)
            sp.dma_start(bv_rep[:], bass.AP(bv.tensor, 0, [[0, P], [1, P]])).then_inc(s_small, 16)
            sp.dma_start(bo_rep[:], bass.AP(bo.tensor, 0, [[0, P], [1, P]])).then_inc(s_small, 16)
            step(None, None, None, 0)
            step(None, None, 0, 1)
            step(None, 0, 1, 2)
            load_rest()
            run_steps(sp, step)
            store(NG - 2)
            store(NG - 1)
            sp.wait_ge(s_out, 16 * NG)

        @block.tensor
        def _(pe):
            mm = nc.tensor.matmul

            def keep_clock(n):
                for _ in range(n):
                    nc.tensor.transpose(ps_up[1][:, 0, 0:P], ident[:], ident[:])

            def project_x(p):
                pe.wait_ge(xn_sb, p + 1)
                for b in range(NB):
                    last = nc.tensor.transpose(ps_xT[:, b * P:(b + 1) * P], xn[:, b, :], ident[:])
                last.then_inc(xT_mm, 1)

            def project_q(p):
                pe.wait_ge(xT_sb, p + 1)
                if at_start(p):
                    pe.wait_ge(dve_setup, 2)
                    pe.wait_ge(s_wqkvo, 32)
                mm(ps_qk[:, 0:T], wT[:, 0, :], xnT[:], start=True, stop=True)

            def project_k(p):
                if at_start(p):
                    pe.wait_ge(s_ctx, 16)
                elif isinstance(p, int) and p == 2:
                    pe.wait_ge(s_ctx, 32)
                mm(ps_qk[:, T:2 * T], wT[:, 1, :], ctx_all[:, bass.ds(p * T, T)], start=True, stop=True).then_inc(qk_mm, 1)

            def project_v(p):
                pe.wait_ge(ctx_sb, p + 1)
                if not at_start(p):
                    pe.wait_ge(max_sb, 2 * NHG * p)
                if isinstance(p, int) and p == 2:
                    pe.wait_ge(s_ctx_rest, 16)
                for b in range(NB):
                    last = mm(ps_v[:, b * P:(b + 1) * P], ctx_g[:, b * P:(b + 1) * P], wT[:, 2, :], start=True, stop=True)
                last.then_inc(v_mm, 1)

            def scores(a, b, g):
                bank, n = ps_s[g % 2], 2 * NHG * a + NHG * b + g
                if b == 0 and g == 0:
                    pe.wait_ge(s_stack, 64 * a + 64)
                    if at_start(a):
                        pe.wait_ge(s_dist, 16)
                        pe.wait_ge(act_setup, 1)
                        pe.wait_ge(own, 8)
                        pe.wait_ge(stack_pads, 2)
                elif b == 0 and g == 1:
                    pe.wait_ge(v_sb, a + 1)
                else:
                    pe.wait_ge(max_sb, n - 1)
                if g == 0:
                    mm(bank[:], dist16[:], slope_hi[:, 0:HG, :], start=True, stop=False, skip_group_check=True)
                for h in range(HG * g, HG * g + HG):
                    o = (h - HG * g) * P
                    last = mm(bank[:, o:o + P], qs[0:ZROWS, h, b * P:(b + 1) * P], ks[0:ZROWS, h, b * P:(b + 1) * P],
                              start=(g > 0), stop=True, skip_group_check=True)
                last.then_inc(s_mm, 1)

            def shift_T(a, b):
                pe.wait_ge(ns_sb, 2 * a + b + 1)
                if b == 1:
                    pe.wait_ge(nm_sb, 2 * a + 1)
                nc.tensor.transpose(ps_nm, nsplit[:, b, :, :].rearrange("p s h -> p (s h)"), ident16[:]).then_inc(nm_mm, 1)

            def scores_T(a, b, g, f=None, p=None):
                bank = ps_st[g % 2]
                if f is not None:
                    pe.wait_ge(lsh_sb, f + 1)
                if p is not None:
                    pe.wait_ge(qklo_sb, 2 * p + 2)
                if at_start(a) and b == 0:
                    if g >= 2:
                        pe.wait_ge(exp_sb, g - 1)
                else:
                    pe.wait_ge(exp_sb, 2 * NHG * a + NHG * b + g - 1)
                if g == 0:
                    pe.wait_ge(s_nm[b], 16 * a + 16)
                    if at_start(a):
                        pe.wait_ge(act_setup, 2)
                        pe.wait_ge(stack_pads, 3)
                h0, first = HG * g, True
                n_split = min(max(SPLIT_SLOPES - h0, 0), HG)
                n_small = min(max(SPLIT_SLOPES + SMALL_SLOPES - h0, 0), HG) - n_split
                if n_split:
                    for part in (slope_hi, slope_lo):
                        mm(bank[:, 0:n_split * P], dist16[:], part[:, h0:h0 + n_split, :], start=first, stop=False,
                           skip_group_check=True)
                        first = False
                if n_small:
                    j = h0 + n_split - SPLIT_SLOPES
                    mm(bank[:, n_split * P:(n_split + n_small) * P], dist16[:], slope_small[:, j:j + n_small, :],
                       start=first, stop=False, skip_group_check=True)
                    first = False
                for h in range(h0, h0 + HG):
                    o = (h - h0) * P
                    last = mm(bank[:, o:o + P], ks[:, h, b * P:(b + 1) * P], qs[:, h, b * P:(b + 1) * P],
                              start=first, stop=True, skip_group_check=True)
                    first = False
                last.then_inc(st_mm, 1)

            def weigh_values(a, b, f=None):
                pe.wait_ge(exp_sb, 2 * NHG * a + NHG * (b + 1))
                if b == 0:
                    pe.wait_ge(v_sb, a + 1)
                    pe.wait_ge(nm_sb, 2 * a + 2)
                if f is not None:
                    pe.wait_ge(cwT_sb, f + 1)
                if not (at_start(a) and b == 0):
                    pe.wait_ge(attn_sb, 2 * a + b)
                for r in range(2):
                    n = (3, 1)[r]
                    for c in range(4):
                        h = 3 * c if r == 0 else 12 + c
                        last = mm(ps_pv[32 * c:32 * c + 32, r * 3 * P:(r * 3 + n) * P], v_aug[:, b, r, c, :],
                                  probs[:, b, h * P:(h + n) * P], start=True, stop=True, skip_group_check=True)
                last.then_inc(pv_mm, 1)

            def values_T(a, b):
                pe.wait_ge(pvev_sb, 2 * a + b + 1)
                for l in range(4):
                    last = nc.tensor.transpose(ps_pv[:, l * P:(l + 1) * P], pv_sb[:, l * P:(l + 1) * P], ident[:])
                last.then_inc(pvT_mm, 1)

            def attention_T(a, b, f):
                pe.wait_ge(attn_sb, 2 * a + b + 1)
                if not (at_start(a) and b == 0):
                    pe.wait_ge(x1_sb, 2 * a + b)
                if f is not None and not at_start(f):
                    pe.wait_ge(y_sb, f)
                nc.tensor.transpose(ps_aT, attn[:], ident[:]).then_inc(aT_mm, 1)

            def project_out(a, b):
                pe.wait_ge(aT_sb, 2 * a + b + 1)
                mm(ps_o, attnT[:], wT[:, 3, :], start=True, stop=True).then_inc(o_mm, 1)

            def expert_in_T(f):
                pe.wait_ge(x2n_sb, NB * f + NB)
                for b in range(NB):
                    last = nc.tensor.transpose(ps_x2T[:, b * P:(b + 1) * P], x2n[:, b, :], ident[:])
                last.then_inc(x2T_mm, 1)

            def router(f):
                for b in range(NB):
                    for n, (u, w) in enumerate(((x2_lo, wr_hi), (x2_hi, wr_lo), (x2_hi, wr_hi))):
                        last = mm(ps_lg[:, b * E:(b + 1) * E], u[:, b * P:(b + 1) * P], w[:], start=(n == 0), stop=(n == 2))
                last.then_inc(lg_mm, 1)

            def weights_T(f, a):
                pe.wait_ge(cw_sb, f + 1)
                if a is not None:
                    pe.wait_ge(nm_sb, 2 * a + 2)
                for b in range(NB):
                    last = nc.tensor.transpose(ps_cwT[:, b * P:(b + 1) * P], cw[:, b, :], ident[:])
                last.then_inc(cwT_mm, 1)

            def up(f, c):
                if c == 0:
                    pe.wait_ge(x2hi_sb, f + 1)
                    if at_start(f):
                        pe.wait_ge(act_setup, 5)
                        pe.wait_ge(dve_setup, 5)
                if not (at_start(f) and c < 2):
                    pe.wait_ge(hid_sb, NCH * f + max(c - 1, 0))
                gate_up = ((wg_hi, wg_lo), (wu_hi, wu_lo))
                for k, weights in enumerate(gate_up):
                    for n, w in enumerate(weights):
                        mm(ps_up[c % 2][:, k, :], w[:, c, :], x2_hi[:], start=(k == 0 and n == 0), stop=False,
                           skip_group_check=True)
                if c == 0:
                    pe.wait_ge(x2lo_sb, f + 1)
                for k, (hi, _) in enumerate(gate_up):
                    last = mm(ps_up[c % 2][:, k, :], hi[:, c, :], x2_lo[:], start=False, stop=True, skip_group_check=True)
                last.then_inc(up_mm, 1)

            def down(f, chunks, out_product=None, weighted_sb=None):
                for c in chunks:
                    if c == 0:
                        if at_start(f):
                            pe.wait_ge(pool_setup, 1)
                        elif out_product is None:
                            pe.wait_ge(y_sb, f)
                        if out_product is not None:
                            pe.wait_ge(x1_sb, 2 * out_product + 2)
                    if c == SHARED:
                        pe.wait_ge(hid_sb, NCH * f + NCH)
                    elif weighted_sb is not None:
                        pe.wait_ge(weighted_sb, c + 1)
                    elif c % 2 == 0:
                        pe.wait_ge(hc_sb, PAIRS * f + c // 2 + 1)
                    for b in range(NB):
                        last = mm(ps_dn[:, b * P:(b + 1) * P], hid[:, c, b * P:(b + 1) * P], wd_sb[:, c, :],
                                  start=(c == 0 and b == 0), stop=(c == SHARED), skip_group_check=True)
                    last.then_inc(dn_mm, 1)

            def step(f, a, p, q):
                fs, as_, ps, qs_ = f is not None, a is not None, p is not None, q is not None

                def late_down(*chunks):
                    if fs and not at_start(f): down(f - 1, chunks, f)

                if as_: scores(a, 0, 0)
                if as_: scores(a, 0, 1)
                late_down(0, 1)
                if ps: project_q(p)
                if as_: scores(a, 0, 2)
                if fs: expert_in_T(f)
                if ps: project_k(p)
                if as_: scores(a, 0, 3)
                late_down(2)
                if fs: up(f, 0)
                if as_: scores(a, 1, 0)
                if fs: up(f, 1)
                if as_:
                    scores(a, 1, 1)
                    shift_T(a, 0)
                if fs: router(f)
                late_down(3)
                if as_: scores(a, 1, 2)
                if fs: up(f, 2)
                late_down(4)
                if as_: scores(a, 1, 3)
                if fs: up(f, 3)
                late_down(5)
                if as_:
                    if not fs: keep_clock(14)
                    scores_T(a, 0, 0, f=f)
                late_down(6)
                if as_:
                    shift_T(a, 1)
                    scores_T(a, 0, 1, p=p)
                late_down(7)
                if fs: up(f, 4)
                if as_: scores_T(a, 0, 2)
                late_down(8)
                if fs: weights_T(f, a)
                if as_: scores_T(a, 0, 3)
                if fs: up(f, 5)
                if as_:
                    scores_T(a, 1, 0)
                    weigh_values(a, 0, f)
                    scores_T(a, 1, 1)
                    values_T(a, 0)
                    scores_T(a, 1, 2)
                if fs: up(f, 6)
                if ps and not at_start(p):
                    pe.wait_ge(pairs_sb, 3 * p)
                if as_:
                    scores_T(a, 1, 3)
                    attention_T(a, 0, f)
                if fs: up(f, 7)
                if as_:
                    weigh_values(a, 1)
                    project_out(a, 0)
                if ps: project_v(p)
                if as_: values_T(a, 1)
                if fs: up(f, 8)
                if as_:
                    attention_T(a, 1, f)
                if qs_: project_x(q)
                if as_: project_out(a, 1)

            pe.wait_ge(s_ident, 16)
            keep_clock(11)
            project_x(0)
            keep_clock(4)
            project_q(0)
            project_k(0)
            keep_clock(5)
            project_v(0)
            keep_clock(5)
            project_x(1)
            keep_clock(10)
            step(None, 0, 1, 2)
            run_steps(pe, step)
            f = NG - 1

            def spread(*chunks):
                for c in chunks:
                    mm(ps_spread[c], select_r[:, c, :], cwT_hi[:], start=True, stop=False, skip_group_check=True)
                    last = mm(ps_spread[c], select_r[:, c, :], cwT_lo[:], start=False, stop=True, skip_group_check=True)
                last.then_inc(spread_mm, 1)

            down(f - 1, (0, 1, 2, 3), f)
            expert_in_T(f)
            up(f, 0)
            router(f)
            up(f, 1)
            down(f - 1, (4,))
            up(f, 2)
            down(f - 1, (5,))
            up(f, 3)
            down(f - 1, (6,))
            weights_T(f, None)
            up(f, 4)
            down(f - 1, (7,))
            pe.wait_ge(cwT_sb, f + 1)
            pe.wait_ge(cwTlo_sb, 1)
            pe.wait_ge(select_sb, 1)
            spread(0, 1)
            up(f, 5)
            down(f - 1, (8,))
            spread(2, 3)
            up(f, 6)
            spread(4, 5)
            down(f, (0,), weighted_sb=hw_sb)
            up(f, 7)
            spread(6, 7)
            down(f, (1,), weighted_sb=hw_sb)
            up(f, 8)
            down(f, range(2, NCH), weighted_sb=hw_sb)

        @block.scalar
        def _(act):
            fn = nc.scalar.activation

            def x_T(p):
                act.wait_ge(xT_mm, p + 1)
                fn(xnT[:], ps_xT, ACT.Copy).then_inc(xT_sb, 1)

            def qk_high(p):
                act.wait_ge(qk_mm, p + 1)
                if at_start(p):
                    act.wait_ge(dve_setup, 2)
                else:
                    act.wait_ge(s_stack, 64 * p)
                for k in range(2):
                    fn(qk_parts[:, 0, k, :], ps_qk[:, k * T:(k + 1) * T], ACT.Identity, bias=bqk_sb[:, k:k + 1]).then_inc(qkhi_sb, 1)

            def shift_copy(a, b):
                act.wait_ge(nm_mm, 2 * a + b + 1)
                if not at_start(a):
                    act.wait_ge(s_nm[b], 16 * a)
                fn(nmT[:, b, :], ps_nm, ACT.Copy).then_inc(nm_sb, 1)

            def exponential(a, b, g):
                act.wait_ge(st_mm, 2 * NHG * a + NHG * b + g + 1)
                if g == 0 and not at_start(a):
                    act.wait_ge(pv_mm, 2 * a + b - 1)
                fn(probs[:, b, g * HG * P:(g + 1) * HG * P], ps_st[g % 2][:], ACT.Exp).then_inc(exp_sb, 1)

            def values_copy(a, b):
                act.wait_ge(pv_mm, 2 * a + b + 1)
                if not (at_start(a) and b == 0):
                    act.wait_ge(pvT_mm, 2 * a + b)
                fn(pv_sb[:], ps_pv[:], ACT.Copy).then_inc(pvev_sb, 1)

            def attention_copy(a, b):
                act.wait_ge(aT_mm, 2 * a + b + 1)
                if not (at_start(a) and b == 0):
                    act.wait_ge(o_mm, 2 * a + b)
                fn(attnT[:], ps_aT, ACT.Copy).then_inc(aT_sb, 1)

            def x2_high(f):
                act.wait_ge(x2T_mm, f + 1)
                if not at_start(f):
                    act.wait_ge(up_mm, NCH * f)
                fn(x2_hi[:], ps_x2T, ACT.Copy).then_inc(x2hi_sb, 1)

            def router_exp(f):
                act.wait_ge(lsh_sb, f + 1)
                if not at_start(f):
                    act.wait_ge(route_sb, ROUTE * f)
                fn(le[:], lsh[:], ACT.Exp).then_inc(lexp_sb, 1)

            def weights_copy(f):
                act.wait_ge(cwT_mm, f + 1)
                if not at_start(f):
                    act.wait_ge(s_cwd, 16 * f)
                fn(cwT[:], ps_cwT, ACT.Copy).then_inc(cwT_sb, 1)

            def tanh(f, c):
                act.wait_ge(up_mm, NCH * f + c + 1)
                if not (at_start(f) and c < 2):
                    act.wait_ge(tg_sb, NCH * f + max(c - 1, 0))
                fn(th[:, c % 2, :], ps_up[c % 2][:, 0, :], ACT.Tanh, scale=0.5).then_inc(tanh_sb, 1)

            def up_weights_high():
                act.wait_ge(s_wu, 16)
                fn(wu_hi[:], wu_sb[:], ACT.Copy).then_inc(act_setup, 1)

            def step(f, a, p, q):
                fs, as_, ps, qs_ = f is not None, a is not None, p is not None, q is not None
                if fs: x2_high(f)
                if ps: qk_high(p)
                if fs:
                    tanh(f, 0)
                    tanh(f, 1)
                if as_:
                    shift_copy(a, 0)
                    if at_start(a): up_weights_high()
                if fs:
                    tanh(f, 2)
                    router_exp(f)
                    tanh(f, 3)
                if as_:
                    exponential(a, 0, 0)
                    shift_copy(a, 1)
                    exponential(a, 0, 1)
                if fs: tanh(f, 4)
                if as_: exponential(a, 0, 2)
                if fs: weights_copy(f)
                if as_: exponential(a, 0, 3)
                if fs: tanh(f, 5)
                if as_:
                    exponential(a, 1, 0)
                    values_copy(a, 0)
                    exponential(a, 1, 1)
                    exponential(a, 1, 2)
                    exponential(a, 1, 3)
                if fs: tanh(f, 6)
                if as_: attention_copy(a, 0)
                if fs: tanh(f, 7)
                if as_:
                    values_copy(a, 1)
                    attention_copy(a, 1)
                if qs_: x_T(q)
                if fs: tanh(f, 8)

            nc.scalar.preload_act_table(ACT.Exp)
            act.wait_ge(s_x, 16)
            x_T(0)
            act.wait_ge(s_ctx, 16)
            act.dma_start(wg_sb[:], wgT).then_inc(s_wg, 16)
            act.dma_start(wr_sb[:], wr).then_inc(s_wg, 16)
            qk_high(0)
            act.wait_ge(s_ident, 16)
            for h in range(SPLIT_SLOPES):
                last = fn(slope_hi[:, h, :], ident[:], ACT.Copy, scale=float(m_hi[h]))
            last.then_inc(act_setup, 1)
            x_T(1)
            for h in range(SPLIT_SLOPES):
                fn(slope_lo[:, h, :], ident[:], ACT.Copy, scale=float(m_lo[h]))
            for j in range(SMALL_SLOPES):
                last = fn(slope_small[:, j, :], ident[:], ACT.Copy, scale=float(m[SPLIT_SLOPES + j]))
            last.then_inc(act_setup, 1)
            act.wait_ge(s_stack, 64)
            act.dma_start(wu_sb[:], wuT).then_inc(s_wu, 16)
            act.wait_ge(s_wg, 32)
            fn(wg_hi[:], wg_sb[:], ACT.Copy).then_inc(act_setup, 1)
            fn(wr_hi[:], wr_sb[:], ACT.Copy).then_inc(act_setup, 1)
            step(None, 0, 1, 2)
            run_steps(act, step)
            f = NG - 1
            act.wait_ge(s_select, 16)
            fn(select_r[:], select[:], ACT.Copy).then_inc(select_sb, 1)
            x2_high(f)
            tanh(f, 0)
            router_exp(f)
            tanh(f, 1)
            tanh(f, 2)
            tanh(f, 3)
            act.wait_ge(cwT_mm, f + 1)
            fn(cwT_hi[:], ps_cwT, ACT.Copy).then_inc(cwT_sb, 1)
            for c in range(4, NCH):
                tanh(f, c)

        @block.vector
        def _(dve):
            v = nc.vector

            def carry_wait():
                v.memset(carrier[:], 0.0)

            def norm1_stats(p):
                if at_start(p):
                    dve.wait_ge(s_x, 16)
                elif isinstance(p, int) and p == 2:
                    dve.wait_ge(s_x, 32)
                elif isinstance(p, int) and p == 3:
                    dve.wait_ge(s_x_rest, 16)
                for b in range(NB):
                    v.bn_stats(stats1[:, b, :], x_all[:, p * NB + b, :]).then_inc(st1_sb, 1)

            def norm1_mean(p):
                dve.wait_ge(st1_sb, NB * p + NB)
                if not at_start(p):
                    dve.wait_ge(ve1_sb, p)
                carry_wait()
                for b in range(NB):
                    v.bn_aggr(mv1[:, b, :], stats1[:, b, :]).then_inc(mv1_sb, 1)

            def norm1(p):
                dve.wait_ge(rstd1_sb, p + 1)
                dve.wait_ge(mv1_sb, NB * p + NB)
                if not at_start(p):
                    dve.wait_ge(xT_mm, p)
                for b in range(NB):
                    last = v.tensor_scalar(xn[:, b, :], x_all[:, p * NB + b, :], mv1[:, b, 0:1], rstd1[:, b:b + 1],
                                           ALU.subtract, ALU.mult)
                last.then_inc(xn_sb, 1)

            def qk_low(p, k):
                dve.wait_ge(qkhi_sb, 2 * p + 2)
                if not at_start(p):
                    dve.wait_ge(s_stack, 64 * p)
                v.scalar_tensor_tensor(out=qk_parts[:, 1, k, :], in0=ps_qk[:, k * T:(k + 1) * T], scalar=bqk_sb[:, k:k + 1],
                                       in1=qk_parts[:, 0, k, :], op0=ALU.add, op1=ALU.subtract).then_inc(qklo_sb, 1)

            def pair_first_parts():
                dve.wait_ge(qklo_sb, 2)
                v.tensor_copy(qk_parts[:, 2:4, 1, :], qk_parts[:, 0:2, 1, :]).then_inc(first_pairs, 1)
                for i in range(2):
                    v.tensor_copy(qk_parts[:, 2 + i, 0, :], qk_parts[:, 1 - i, 0, :]).then_inc(first_pairs, 1)

            def values(p):
                dve.wait_ge(v_mm, p + 1)
                if at_start(p):
                    dve.wait_ge(s_small, 32)
                else:
                    dve.wait_ge(pv_mm, 2 * p)
                for b in range(NB):
                    for r, (h0, n) in enumerate(((0, 3), (12, 1))):
                        w = n * DH
                        src = ps_v[:, b * P + h0 * DH:b * P + h0 * DH + 4 * w].rearrange("p (c w) -> p c w", c=4)
                        bias = bv_rep[:, h0 * DH:h0 * DH + 4 * w].rearrange("p (c w) -> p c w", c=4)
                        last = v.tensor_tensor(v_aug[:, b, r, :, 0:w], src, bias, ALU.add)
                last.then_inc(v_sb, 1)

            def row_max(a, b, g):
                dve.wait_ge(s_mm, 2 * NHG * a + NHG * b + g + 1)
                v.tensor_reduce(nmax[:, b, HG * g:HG * g + HG], ps_s[g % 2][:].rearrange("p (h j) -> p h j", h=HG), AX_X, ALU.max,
                                negate=True).then_inc(max_sb, 1)

            def max_high(a, b):
                dve.wait_ge(max_sb, 2 * NHG * a + NHG * (b + 1))
                v.tensor_copy(nsplit[:, b, 0, :], nmax[:, b, :]).then_inc(nh_sb, 1)

            def max_low(a, b):
                dve.wait_ge(nh_sb, 2 * a + b + 1)
                v.tensor_tensor(nsplit[:, b, 1, :], nmax[:, b, :], nsplit[:, b, 0, :], ALU.subtract).then_inc(ns_sb, 1)

            def row_sums(a, b):
                dve.wait_ge(pvT_mm, 2 * a + b + 1)
                row = ps_pv[:].ap[0]
                v.reciprocal(rden[:], bass.AP(ps_pv, 24, [list(row), [P, 4], [32, 4]])).then_inc(rden_sb, 1)

            def normalise(a, b):
                row = ps_pv[:].ap[0]
                dve.wait_ge(rden_sb, 2 * a + b + 1)
                if not (at_start(a) and b == 0):
                    dve.wait_ge(aT_mm, 2 * a + b)
                v.tensor_tensor(attn[:, 0:96].rearrange("p (c l d) -> p l c d", c=4, l=3),
                                bass.AP(ps_pv, 0, [list(row), [P + DH, 3], [32, 4], [1, DH]]),
                                rden[:, 0:3, :].unsqueeze(3).to_broadcast([P, 3, 4, DH]), ALU.mult)
                v.tensor_tensor(attn[:, 96:128].rearrange("p (c d) -> p c d", c=4),
                                bass.AP(ps_pv, 3 * P, [list(row), [32, 4], [1, DH]]),
                                rden[:, 3, :].unsqueeze(2).to_broadcast([P, 4, DH]), ALU.mult).then_inc(attn_sb, 1)

            def residual1(a, b):
                dve.wait_ge(o_mm, 2 * a + b + 1)
                dve.wait_ge(xb_sb, a + 1)
                v.tensor_tensor(x1_all[:, a * NB + b, :], ps_o, xb[:, b, :], ALU.add).then_inc(x1_sb, 1)

            def norm2_stats(a, b):
                dve.wait_ge(x1_sb, 2 * a + b + 1)
                carry_wait()
                v.bn_stats(stats2[:, b, :], x1_all[:, a * NB + b, :]).then_inc(st2_sb, 1)

            def norm2_mean(a, b):
                dve.wait_ge(st2_sb, 2 * a + b + 1)
                if not at_start(a):
                    dve.wait_ge(ve2_sb, 2 * a + b - 1)
                carry_wait()
                v.bn_aggr(mv2[:, b, :], stats2[:, b, :]).then_inc(mv2_sb, 1)

            def norm2(a, b):
                dve.wait_ge(rstd2_sb, 2 * a + b + 1)
                dve.wait_ge(mv2_sb, 2 * a + b + 1)
                if not at_start(a):
                    dve.wait_ge(x2T_mm, a)
                v.tensor_scalar(x2n[:, b, :], x1_all[:, a * NB + b, :], mv2[:, b, 0:1], rstd2[:, b:b + 1],
                                ALU.subtract, ALU.mult).then_inc(x2n_sb, 1)

            def x2_low(f):
                dve.wait_ge(x2hi_sb, f + 1)
                if not at_start(f):
                    dve.wait_ge(up_mm, NCH * f)
                v.tensor_tensor(x2_lo[:], ps_x2T, x2_hi[:].bitcast(F32), ALU.subtract).then_inc(x2lo_sb, 1)

            logits = ps_lg.rearrange("p (b e) -> p b e", b=NB)

            def router_max(f):
                dve.wait_ge(lg_mm, f + 1)
                v.tensor_reduce(lmax[:], logits, AX_X, ALU.max).then_inc(lmax_sb, 1)

            def router_shift(f):
                if not at_start(f):
                    dve.wait_ge(lexp_sb, f)
                dve.wait_ge(lmax_sb, f + 1)
                v.tensor_tensor(lsh[:], logits, lmax[:].unsqueeze(2).to_broadcast([P, NB, E]), ALU.subtract).then_inc(lsh_sb, 1)

            def route(f, i):
                if i == 0:
                    dve.wait_ge(lexp_sb, f + 1)
                else:
                    dve.wait_ge(route_sb, ROUTE * f + i)
                if i == 0:
                    last = v.tensor_reduce(lsum[:], le[:], AX_X, ALU.add)
                elif i == 1:
                    last = v.reciprocal(lrec[:], lsum[:])
                elif i == 2:
                    last = v.tensor_tensor(pr[:, :, 0:E], le[:], lrec[:].unsqueeze(2).to_broadcast([P, NB, E]), ALU.mult)
                elif i == 3:
                    carry_wait()
                    for b in range(NB):
                        last = v.max(top8[:, b, :], pr[:, b, 0:E])
                elif i == 4:
                    last = v.tensor_copy(drop8[:, :, 0:2], top8[:, :, 0:2])
                elif i == 5:
                    carry_wait()
                    for b in range(NB):
                        last = v.match_replace(rest[:, b, :], drop8[:, b, :], pr[:, b, :], 0.0)
                else:
                    if not at_start(f):
                        dve.wait_ge(cwT_mm, f)
                    v.tensor_tensor(cw[:], pr[:, :, 0:E], rest[:, :, 0:E], ALU.subtract).then_inc(cw_sb, 1)
                    return
                last.then_inc(route_sb, 1)

            def gate(f, c):
                dve.wait_ge(tanh_sb, NCH * f + c + 1)
                v.scalar_tensor_tensor(out=tg[:, c % 2, :], in0=th[:, c % 2, :], scalar=1.0, in1=ps_up[c % 2][:, 0, :],
                                       op0=ALU.add, op1=ALU.mult).then_inc(tg_sb, 1)

            def hidden(f, c):
                dve.wait_ge(tg_sb, NCH * f + c + 1)
                v.tensor_tensor(hid[:, c, :], tg[:, c % 2, :], ps_up[c % 2][:, 1, :], ALU.mult).then_inc(hid_sb, 1)

            def residual2(f):
                dve.wait_ge(dn_mm, NCH * f + NCH)
                x1 = x1_all[:, bass.ds(f * NB, NB), :]
                v.tensor_tensor(x1, ps_dn.rearrange("p (b d) -> p b d", b=NB), x1, ALU.add).then_inc(y_sb, 1)

            def weights_low():
                dve.wait_ge(act_setup, 5)
                v.tensor_tensor(wg_lo[:], wg_sb[:], wg_hi[:].bitcast(F32), ALU.subtract).then_inc(dve_setup, 1)
                v.tensor_tensor(wu_lo[:], wu_sb[:], wu_hi[:].bitcast(F32), ALU.subtract).then_inc(dve_setup, 1)
                v.tensor_tensor(wr_lo[:], wr_sb[:], wr_hi[:].bitcast(F32), ALU.subtract).then_inc(dve_setup, 1)

            def step(f, a, p, q):
                fs, as_, ps, qs_ = f is not None, a is not None, p is not None, q is not None
                late = fs and not at_start(f)
                if as_: row_max(a, 0, 0)
                if late: gate(f - 1, 8)
                if fs: norm2(f, 1)
                if late: hidden(f - 1, 8)
                if as_:
                    row_max(a, 0, 1)
                    row_max(a, 0, 2)
                if fs: x2_low(f)
                if as_:
                    row_max(a, 0, 3)
                    max_high(a, 0)
                if fs: gate(f, 0)
                if as_: max_low(a, 0)
                if fs: hidden(f, 0)
                if as_: row_max(a, 1, 0)
                if fs: gate(f, 1)
                if as_: row_max(a, 1, 1)
                if fs:
                    hidden(f, 1)
                    router_max(f)
                if as_: row_max(a, 1, 2)
                if fs: router_shift(f)
                if ps: qk_low(p, 0)
                if fs: gate(f, 2)
                if ps:
                    qk_low(p, 1)
                if fs: hidden(f, 2)
                if as_: row_max(a, 1, 3)
                if fs: route(f, 0)
                if as_: max_high(a, 1)
                if fs: route(f, 1)
                if as_: max_low(a, 1)
                if fs:
                    route(f, 2)
                    gate(f, 3)
                    route(f, 3)
                    hidden(f, 3)
                    route(f, 4)
                if as_ and at_start(a): weights_low()
                if qs_ and fs: norm1_stats(q)
                if fs:
                    route(f, 5)
                    route(f, 6)
                    gate(f, 4)
                if qs_ and fs: norm1_mean(q)
                if fs:
                    hidden(f, 4)
                    if late: residual2(f - 1)
                    gate(f, 5)
                if qs_ and fs: norm1(q)
                if fs: hidden(f, 5)
                if as_:
                    row_sums(a, 0)
                    normalise(a, 0)
                if qs_ and not fs:
                    norm1_stats(q)
                    norm1_mean(q)
                    if as_: residual1(a, 0)
                    norm1(q)
                if fs:
                    gate(f, 6)
                    hidden(f, 6)
                if fs: gate(f, 7)
                if as_ and not (qs_ and not fs): residual1(a, 0)
                if fs: hidden(f, 7)
                if as_:
                    norm2_stats(a, 0)
                    row_sums(a, 1)
                    norm2_mean(a, 0)
                    normalise(a, 1)
                if ps: values(p)
                if as_:
                    norm2(a, 0)
                    residual1(a, 1)
                    norm2_stats(a, 1)
                    norm2_mean(a, 1)

            v.memset(stacks_sb[2 * SROWS:ZROWS, 0:H // 2].bitcast(F32), 0.0).then_inc(stack_pads, 1)
            step(None, None, None, 0)
            dve.wait_ge(s_wqkvo, 32)
            v.tensor_scalar(wT[:, 0, :], wT[:, 0, :], q_scale, None, ALU.mult).then_inc(dve_setup, 1)
            v.tensor_scalar(bqk_sb[:, 0:1], bqk_sb[:, 0:1], q_scale, None, ALU.mult).then_inc(dve_setup, 1)
            v.memset(stacks_sb[2 * SROWS:ZROWS, H // 2:].bitcast(F32), 0.0).then_inc(stack_pads, 1)
            norm1_stats(1)
            norm1_mean(1)
            qk_low(0, 0)
            qk_low(0, 1)
            pair_first_parts()
            norm1(1)
            v.memset(ks[ZROWS:AROWS].bitcast(F32), two_ones).then_inc(stack_pads, 1)
            values(0)
            step(None, 0, 1, 2)
            run_steps(dve, step)
            f = NG - 1

            def weigh_chunk(c):
                dve.wait_ge(spread_mm, c // 2 + 1)
                dve.wait_ge(hid_sb, NCH * f + c + 1)
                v.tensor_tensor(hid[:, c, :], hid[:, c, :], ps_spread[c], ALU.mult).then_inc(hw_sb, 1)

            gate(f - 1, 8)
            norm2(f, 1)
            hidden(f - 1, 8)
            x2_low(f)
            gate(f, 0)
            router_max(f)
            hidden(f, 0)
            router_shift(f)
            gate(f, 1)
            route(f, 0)
            hidden(f, 1)
            for i in range(1, 4):
                route(f, i)
            gate(f, 2)
            route(f, 4)
            hidden(f, 2)
            route(f, 5)
            route(f, 6)
            gate(f, 3)
            hidden(f, 3)
            dve.wait_ge(cwT_sb, f + 1)
            v.tensor_tensor(cwT_lo[:], ps_cwT, cwT_hi[:].bitcast(F32), ALU.subtract).then_inc(cwTlo_sb, 1)
            gate(f, 4)
            hidden(f, 4)
            weigh_chunk(0)
            gate(f, 5)
            residual2(f - 1)
            hidden(f, 5)
            weigh_chunk(1)
            gate(f, 6)
            weigh_chunk(2)
            hidden(f, 6)
            weigh_chunk(3)
            gate(f, 7)
            weigh_chunk(4)
            hidden(f, 7)
            weigh_chunk(5)
            gate(f, 8)
            weigh_chunk(6)
            hidden(f, 8)
            weigh_chunk(7)
            residual2(f)

        @block.gpsimd
        def _(pool):
            g = nc.gpsimd

            def carry_wait(place):
                g.tensor_tensor(pool_carrier[:, place:place + 1], neg_half[:, 0:1], neg_half[:, 0:1], ALU.add)

            def inverse_deviation1(q):
                pool.wait_ge(mv1_sb, NB * q + NB)
                g.tensor_tensor(ve1[:], mv1[:, :, 1], eps_sb[:], ALU.add).then_inc(ve1_sb, 1)
                pool.wait_ge(ve1_sb, q + 1)
                if not at_start(q):
                    pool.wait_ge(xn_sb, q)
                g.tensor_tensor(rstd1[:], ve1[:], neg_half[:], ALU.pow).then_inc(rstd1_sb, 1)

            def inverse_deviation2(a, b):
                pool.wait_ge(mv2_sb, 2 * a + b + 1)
                g.tensor_tensor(ve2[:, b:b + 1], mv2[:, b, 1:2], eps_sb[:, b:b + 1], ALU.add).then_inc(ve2_sb, 1)
                pool.wait_ge(ve2_sb, 2 * a + b + 1)
                if not at_start(a):
                    pool.wait_ge(x2n_sb, 2 * a + b - 1)
                g.tensor_tensor(rstd2[:, b:b + 1], ve2[:, b:b + 1], neg_half[:, b:b + 1], ALU.pow).then_inc(rstd2_sb, 1)

            def add_bo(a):
                if at_start(a):
                    pool.wait_ge(s_small, 32)
                    pool.wait_ge(s_x, 16)
                else:
                    pool.wait_ge(x1_sb, 2 * a)
                for b in range(NB):
                    last = g.tensor_tensor(xb[:, b, :], x_all[:, a * NB + b, :], bo_rep[:], ALU.add)
                last.then_inc(xb_sb, 1)

            def copy_ctx(p):
                if at_start(p):
                    pool.wait_ge(s_ctx, 16)
                else:
                    if isinstance(p, int) and p == 2:
                        pool.wait_ge(s_ctx, 32)
                    pool.wait_ge(v_mm, p)
                carry_wait(0)
                g.tensor_copy(ctx_g[:], ctx_all[:, bass.ds(p * T, T)]).then_inc(ctx_sb, 1)

            def pair_parts(p):
                pool.wait_ge(qkhi_sb, 2 * p + 2)
                pool.wait_ge(qklo_sb, 2 * p + 2)
                pool.wait_ge(s_stack, 64 * p)
                carry_wait(1)
                g.tensor_copy(qk_parts[:, 2:4, 1, :], qk_parts[:, 0:2, 1, :]).then_inc(pairs_sb, 1)
                for i in range(2):
                    g.tensor_copy(qk_parts[:, 2 + i, 0, :], qk_parts[:, 1 - i, 0, :]).then_inc(pairs_sb, 1)

            def weigh_experts(f, pair):
                if pair == 0:
                    pool.wait_ge(s_crep, 32 * f + 32)
                pool.wait_ge(hid_sb, NCH * f + 2 * pair + 2)
                h2, c2 = hid[:, 2 * pair:2 * pair + 2, :], crep[:, 2 * pair:2 * pair + 2, :]
                g.tensor_tensor(h2, h2, c2, ALU.mult).then_inc(hc_sb, 1)

            def step(f, a, p, q):
                if f is not None and not at_start(f):
                    for pair in range(1, PAIRS):
                        weigh_experts(f - 1, pair)
                if p is not None and not at_start(p):
                    pair_parts(p)
                early = q is not None and f is not None
                if early:
                    inverse_deviation1(q)
                if a is not None:
                    add_bo(a)
                if p is not None:
                    copy_ctx(p)
                if q is not None and not early:
                    inverse_deviation1(q)
                if f is not None:
                    weigh_experts(f, 0)
                if a is not None:
                    inverse_deviation2(a, 0)
                    if p is None:
                        weigh_experts(f, 1)
                    inverse_deviation2(a, 1)

            g.memset(neg_half[:], -0.5).then_inc(own, 1)
            g.memset(eps_sb[:], EPS).then_inc(own, 1)
            g.memset(v_aug[:], 1.0).then_inc(own, 1)
            g.memset(pr[:, :, E:], -1.0).then_inc(own, 1)
            g.memset(drop8[:], -1.0).then_inc(own, 1)
            pool.wait_ge(own, 5)
            g.memset(v_aug[:, :, 1, :, DH:3 * DH], 0.0).then_inc(own, 1)
            pool.wait_ge(own, 6)
            step(None, None, None, 0)
            pool.wait_ge(rstd1_sb, 1)
            g.memset(stacks_sb[SROWS:2 * SROWS].bitcast(F32), 0.0).then_inc(own, 1)
            pool.wait_ge(own, 7)
            copy_ctx(0)
            pool.wait_ge(ctx_sb, 1)
            inverse_deviation1(1)
            pool.wait_ge(s_ident, 16)
            pool.wait_ge(rstd1_sb, 2)
            g.tensor_copy(ident16[:], ident[:]).then_inc(own, 1)
            pool.wait_ge(own, 8)
            step(None, 0, 1, 2)
            pool.wait_ge(rstd2_sb, 2)
            pool.wait_ge(s_wd, 16)
            g.tensor_scalar(wd_sb[:], wd_sb[:], 0.5, None, ALU.mult).then_inc(pool_setup, 1)
            pool.wait_ge(pool_setup, 1)
            run_steps(pool, step)
            for pair in range(2, PAIRS):
                weigh_experts(NG - 2, pair)


def kernel(x, ctx_1024, L0_xattn_Wq, L0_xattn_bq, L0_xattn_Wk, L0_xattn_bk, L0_xattn_Wv, L0_xattn_bv, L0_xattn_Wo,
           L0_xattn_bo, L0_ffn_Wr, L0_ffn_Wg, L0_ffn_Wu, L0_ffn_Wd, L0_ffn_Sg, L0_ffn_Su, L0_ffn_Sd):
    import numpy as np
    import concourse.bacc as bacc
    from concourse.bass_utils import run_bass_kernel_spmd

    def rows(a):
        return np.ascontiguousarray(a)

    def by_dim(w):
        return np.asarray(w).reshape(H, DH, -1).transpose(2, 1, 0).reshape(P, P)

    x, ctx = np.asarray(x), np.asarray(ctx_1024)
    B = x.shape[0]
    arrays = {
        "x": rows(x.transpose(1, 0, 2)),
        "ctxT": rows(ctx.transpose(2, 0, 1).reshape(P, B * P)),
        "wqkvoT": rows(np.stack([by_dim(L0_xattn_Wq), by_dim(L0_xattn_Wk), np.asarray(L0_xattn_Wv).T,
                                 np.asarray(L0_xattn_Wo).T], axis=1)),
        "bqk": rows(np.stack([np.asarray(b).reshape(H, DH).T.reshape(P) for b in (L0_xattn_bq, L0_xattn_bk)], axis=1)),
        "bv": rows(L0_xattn_bv), "bo": rows(L0_xattn_bo),
        "wgT": rows(np.concatenate([np.asarray(L0_ffn_Wg).transpose(1, 0, 2).reshape(P, E * FE), np.asarray(L0_ffn_Sg)],
                                   axis=1).reshape(P, NCH, P)),
        "wuT": rows(np.concatenate([np.asarray(L0_ffn_Wu).transpose(1, 0, 2).reshape(P, E * FE), np.asarray(L0_ffn_Su)],
                                   axis=1).reshape(P, NCH, P)),
        "wd": rows(np.concatenate([np.asarray(L0_ffn_Wd).reshape(E * FE, P), np.asarray(L0_ffn_Sd)],
                                  axis=0).reshape(NCH, P, P).transpose(1, 0, 2)),
        "wr": rows(L0_ffn_Wr),
        **constants(),
    }
    nc = bacc.Bacc("TRN2", target_bir_lowering=False, num_devices=1)
    aps = {n: nc.dram_tensor(f"in_{n}", a.shape, mybir.dt.from_np(a.dtype), kind="ExternalInput").ap()
           for n, a in arrays.items()}
    out = nc.dram_tensor("out_y", (P, B, P), F32, kind="ExternalOutput").ap()
    xattn_moe_kernel(nc, out=out, **aps)
    r = run_bass_kernel_spmd(nc, [{f"in_{n}": a for n, a in arrays.items()}], core_ids=[0])
    return r.results[0]["out_y"].transpose(1, 0, 2)
```
